# Optimizing a Trainium2 kernel written in Bass

```python
import numpy as np
import jax
import jax.numpy as jnp

def _softmax(x, axis=-1):
    return jax.nn.softmax(x, axis=axis)

def _gelu(x):
    return jax.nn.gelu(x, approximate=True)

def _silu(x):
    return jax.nn.silu(x)

def _sigmoid(x):
    return jax.nn.sigmoid(x)

def _layernorm(x, axis=-1, eps=1e-05):
    m = jnp.mean(x, axis=axis, keepdims=True)
    v = jnp.var(x, axis=axis, keepdims=True)
    return (x - m) / jnp.sqrt(v + eps)

def _scatter_add(tgt, idx, src, axis=0):
    return tgt.at[idx].add(src)

def _segment_sum(src, seg, n):
    return jax.ops.segment_sum(src, seg, n)
kernel_name = 'mk_seq_postln_d1_jaxref_r4_418f78'

def setup_inputs(seed: int=0):
    np.random.seed(seed)
    _w = jnp.asarray

    def _L0_attn_setup():
        import jax, jax.numpy as jnp
        import numpy as np
        D_HEAD = 64
        MASK_FILL = -1000000.0
        key = jax.random.key(seed)
        ks = jax.random.split(key, 5)
        batch, seq, d_model, n_heads, d_head = (4, 512, 256, 16, D_HEAD)
        bound_qkv = float(np.sqrt(6.0 / (d_model + n_heads * d_head)))
        bound_out = float(np.sqrt(6.0 / (d_head + n_heads * d_model)))
        return {'resid': jax.random.normal(ks[0], (batch, seq, d_model), dtype=jnp.float32), 'W_Q': jax.random.uniform(ks[1], (d_model, n_heads, d_head), jnp.float32, -bound_qkv, bound_qkv), 'W_K': jax.random.uniform(ks[2], (d_model, n_heads, d_head), jnp.float32, -bound_qkv, bound_qkv), 'W_V': jax.random.uniform(ks[3], (d_model, n_heads, d_head), jnp.float32, -bound_qkv, bound_qkv), 'W_out': jax.random.uniform(ks[4], (d_head, n_heads, d_model), jnp.float32, -bound_out, bound_out), 'b_out': jnp.zeros((d_model,), dtype=jnp.float32)}
    _L0_attn_in = _L0_attn_setup()

    def _L0_ffn_setup():
        import jax, jax.numpy as jnp
        import numpy as np
        B, S, H, F, G = (8, 512, 256, 1024, 128)
        EPS = 1e-05

        def _dequant(q, scales, g):
            K, N = q.shape
            w = (q.astype(jnp.float32) - 128.0).reshape(K // g, g, N) * scales[:, None, :]
            return w.reshape(K, N)
        key = jax.random.key(seed)
        ks = jax.random.split(key, 8)
        x = jax.random.normal(ks[0], (B, S, H), dtype=jnp.float32)
        ln_gamma = jnp.ones((H,), jnp.float32)
        ln_beta = jnp.zeros((H,), jnp.float32)
        fc1_q = jax.random.randint(ks[1], (H, F), 0, 64, dtype=jnp.int32)
        fc2_q = jax.random.randint(ks[2], (F, H), 0, 64, dtype=jnp.int32)
        fc1_scales = jax.random.uniform(ks[3], (H // G, F), jnp.float32) * 0.02 + 0.001
        fc2_scales = jax.random.uniform(ks[4], (F // G, H), jnp.float32) * 0.02 + 0.001
        fc1_bias = jax.random.normal(ks[5], (F,), jnp.float32) * 0.02
        fc2_bias = jax.random.normal(ks[6], (H,), jnp.float32) * 0.02
        return {'x': x, 'ln_gamma': ln_gamma, 'ln_beta': ln_beta, 'fc1_q': fc1_q, 'fc1_scales': fc1_scales, 'fc1_bias': fc1_bias, 'fc2_q': fc2_q, 'fc2_scales': fc2_scales, 'fc2_bias': fc2_bias}
    _L0_ffn_in = _L0_ffn_setup()
    _d = {'L0_attn_resid': _L0_attn_in['resid'], 'L0_attn_W_Q': _L0_attn_in['W_Q'], 'L0_attn_W_K': _L0_attn_in['W_K'], 'L0_attn_W_V': _L0_attn_in['W_V'], 'L0_attn_W_out': _L0_attn_in['W_out'], 'L0_attn_b_out': _L0_attn_in['b_out'], 'L0_ffn_ln_gamma': _L0_ffn_in['ln_gamma'], 'L0_ffn_ln_beta': _L0_ffn_in['ln_beta'], 'L0_ffn_fc1_q': _L0_ffn_in['fc1_q'], 'L0_ffn_fc1_scales': _L0_ffn_in['fc1_scales'], 'L0_ffn_fc1_bias': _L0_ffn_in['fc1_bias'], 'L0_ffn_fc2_q': _L0_ffn_in['fc2_q'], 'L0_ffn_fc2_scales': _L0_ffn_in['fc2_scales'], 'L0_ffn_fc2_bias': _L0_ffn_in['fc2_bias']}
    _x0 = _d['L0_attn_resid']
    _d['L0_attn_resid'] = jax.random.normal(jax.random.fold_in(jax.random.key(seed), 1), (2, 2048, 256), dtype=_x0.dtype)
    del _x0
    return _d

def reference(L0_attn_resid, L0_attn_W_Q, L0_attn_W_K, L0_attn_W_V, L0_attn_W_out, L0_attn_b_out, L0_ffn_ln_gamma, L0_ffn_ln_beta, L0_ffn_fc1_q, L0_ffn_fc1_scales, L0_ffn_fc1_bias, L0_ffn_fc2_q, L0_ffn_fc2_scales, L0_ffn_fc2_bias):

    def _L0_attn_ref(resid, W_Q, W_K, W_V, W_out, b_out):
        import jax, jax.numpy as jnp
        import numpy as np
        D_HEAD = 64
        MASK_FILL = -1000000.0
        seq = resid.shape[1]
        d_head = W_Q.shape[-1]
        q = jnp.einsum('bsd,dhk->bshk', resid, W_Q)
        k = jnp.einsum('bsd,dhk->bshk', resid, W_K)
        v = jnp.einsum('bsd,dhk->bshk', resid, W_V)
        scores = jnp.einsum('bqhk,bkhd->bhqd', q, k.astype(q.dtype)) if False else jnp.einsum('bqhc,bshc->bhqs', q, k)
        scores = scores / jnp.sqrt(jnp.asarray(d_head, dtype=scores.dtype))
        causal_mask = jnp.triu(jnp.ones((seq, seq), dtype=bool), k=1)
        scores = jnp.where(causal_mask, MASK_FILL, scores)
        probs = jax.nn.softmax(scores, axis=-1)
        z = jnp.einsum('bhqs,bshc->bqhc', probs, v)
        out = jnp.einsum('bqhc,chd->bqd', z, W_out) + b_out
        return out

    def _L0_ffn_ref(x, ln_gamma, ln_beta, fc1_q, fc1_scales, fc1_bias, fc2_q, fc2_scales, fc2_bias):
        import jax, jax.numpy as jnp
        import numpy as np
        B, S, H, F, G = (8, 512, 256, 1024, 128)
        EPS = 1e-05

        def _dequant(q, scales, g):
            K, N = q.shape
            w = (q.astype(jnp.float32) - 128.0).reshape(K // g, g, N) * scales[:, None, :]
            return w.reshape(K, N)
        residual = x
        mu = jnp.mean(x, axis=-1, keepdims=True)
        var = jnp.mean(jnp.square(x - mu), axis=-1, keepdims=True)
        h = (x - mu) * jax.lax.rsqrt(var + EPS) * ln_gamma + ln_beta
        hf = h.reshape(-1, H)
        w1 = _dequant(fc1_q, fc1_scales, G)
        y = hf @ w1 + fc1_bias
        y = jax.nn.silu(y)
        w2 = _dequant(fc2_q, fc2_scales, G)
        z = y @ w2 + fc2_bias
        return residual + 0.5 * z.reshape(residual.shape)
    x = L0_attn_resid
    x = _layernorm(x + _L0_attn_ref(x, L0_attn_W_Q, L0_attn_W_K, L0_attn_W_V, L0_attn_W_out, L0_attn_b_out), axis=-1)
    x = _layernorm(x + _L0_ffn_ref(x, L0_ffn_ln_gamma, L0_ffn_ln_beta, L0_ffn_fc1_q, L0_ffn_fc1_scales, L0_ffn_fc1_bias, L0_ffn_fc2_q, L0_ffn_fc2_scales, L0_ffn_fc2_bias), axis=-1)
    return x

_drawn_inputs = setup_inputs


def setup_inputs(seed=0):
    import zlib

    import numpy as np

    out = dict(_drawn_inputs(seed))
    spreads = {'L0_attn_b_out': (0.0, 0.8), 'L0_ffn_ln_gamma': (1.0, 0.2), 'L0_ffn_ln_beta': (0.0, 0.1)}
    factors = {'L0_attn_W_Q': 5.286,
     'L0_attn_W_K': 6.896,
     'L0_attn_W_V': 3.309,
     'L0_attn_W_out': 3.902,
     'L0_ffn_fc1_bias': 50.369,
     'L0_ffn_fc2_bias': 200.0}
    for name, (base, spread) in spreads.items():
        noise = np.random.default_rng([zlib.crc32(name.encode()), seed]).standard_normal(out[name].shape)
        drawn = base * np.exp(spread * noise) if base else spread * noise
        out[name] = jnp.asarray(drawn.astype(out[name].dtype))
    for name, factor in factors.items():
        out[name] = (out[name] * factor).astype(out[name].dtype)
    return out
```

```python
from contextlib import ExitStack

import concourse.bass as bass
from concourse import mybir

F32 = mybir.dt.float32
F32R = mybir.dt.float32r
BF16 = mybir.dt.bfloat16
F16 = mybir.dt.float16
I32 = mybir.dt.int32
ALU = mybir.AluOpType
ACT = mybir.ActivationFunctionType
AX = mybir.AxisListType

P = 128
B, S, D = 2, 2048, 256
H, C = 16, 64
F, G = 1024, 128
DT = D // P
FT = F // P
PAIRS = H // 2
ST = S // P
QB = 512
NQ = S // QB
NBLK = 2 * NQ
TPB = QB // P
VW = 3 * C + 1
VS = VW + 1
START = 1
LAG = 3
NP = 5
NEG = -1.0e30
EPS = 1e-5
SCALE = C ** -0.5
SHIFT = 5.545177444479562 / SCALE
TOKB = B * NQ


def block_of(n):
    return n // NQ, n % NQ


SLOTS = [(n, s) for n in range(NBLK) for s in range(2 * (block_of(n)[1] + 1))]
SLOT0 = [min(i for i, (m, _) in enumerate(SLOTS) if m == n) for n in range(NBLK)]
SLOTN = [max(i for i, (m, _) in enumerate(SLOTS) if m == n) for n in range(NBLK)]
NSLOT = len(SLOTS)


def chunks_of(n):
    q = block_of(n)[1]
    return [("chunk", n, t, c) for t in range(TPB) for c in range(q + 1)]


def chunk_width(n, t, c):
    return QB if c < block_of(n)[1] else P * (t + 1)


def slot_tiles(n, s):
    q = block_of(n)[1]
    return [(i, 2 * s + i, max(0, 2 * s + i - TPB * q)) for i in range(2)]


def ring_schedule():
    def width(item):
        return chunk_width(*item[1:]) + 60
    left = [x for n in range(NBLK) for x in chunks_of(n)]
    total = sum(width(x) for x in left)
    tiles = [sum(TPB - f for _, _, f in slot_tiles(n, s)) for n, s in SLOTS]
    done, pending = 0, []
    steps = []

    def emit(until_block, target):
        nonlocal done, pending
        out, pending = pending, []
        while left and (left[0][1] <= until_block or done < target):
            x = left.pop(0)
            out.append(x)
            done += width(x)
            if not left or left[0][1] != x[1]:
                pending.append(("turn", x[1]))
        return out
    ahead = emit(1, 0)
    a, b = [x for x in ahead if x[1] == 0], [x for x in ahead if x[1] == 1]
    ahead = a + b[:1] + [("turn", 0)] + b[1:]
    pending = [x for x in pending if x[1] != 0]
    base = done
    for i in range(NSLOT):
        n_soon = SLOTS[min(i + 3, NSLOT - 1)][0]
        steps.append(emit(n_soon, base + (total - base) * sum(tiles[:i + 1]) / sum(tiles)))
    assert not left and not pending
    return ahead, steps


AHEAD, STEP_RING = ring_schedule()
RING_N = len(AHEAD) + sum(len(x) for x in STEP_RING)
CHUNK_N = len([x for n in range(NBLK) for x in chunks_of(n)])
QK_GROUPS = 2 * NQ
V_GROUPS = ST // TPB
GROUPS = QK_GROUPS + V_GROUPS



def attention(nc, xT, wqkv, zT_dram):
    with ExitStack() as ctx:
        def sb(name, shape, dt=F32):
            return ctx.enter_context(nc.sbuf_tensor(name, shape, dt))

        def sem(name):
            return ctx.enter_context(nc.semaphore(name))

        ident = sb("ident", [P, P])
        ident_b = sb("ident_b", [P, P], BF16)
        mask_q = sb("mask_q", [P, P], BF16)
        mask_k = sb("mask_k", [P, P], BF16)
        row_sel = sb("row_sel", [TPB, TPB, P])
        qa = sb("qa", [P, 2, S], F32R)
        qb = sb("qb", [P, 2, S], F32R)
        ka = sb("ka", [P, 2, S], F32R)
        kb = sb("kb", [P, 2, S], F32R)
        x_raw = sb("x_raw", [P, DT, S])
        x_hi = sb("x_hi", [P, DT, S], F32R)
        x_lo = sb("x_lo", [P, DT, S], F32R)
        w_raw = sb("w_raw", [P, DT, 3 * P])
        w_hi = sb("w_hi", [P, DT, 3 * P], F32R)
        w_lo = sb("w_lo", [P, DT, 3 * P], F32R)
        v3 = sb("v3", [P, ST, 2, VS], BF16)
        v_rest = sb("v_rest", [P, 2, TPB, 2, C])
        p_full = sb("p_full", [P, NP, 2, QB])
        p_hi = sb("p_hi", [P, NP, 2, QB], F16)
        p_lo = sb("p_lo", [P, NP, 2, QB], F16)
        row_max = sb("row_max", [P, 2, TPB, NQ])
        neg_max = sb("neg_max", [P, 2, TPB])
        z_rcp = sb("z_rcp", [P, TPB])
        z_sum = sb("z_sum", [P, TPB, C])
        z_pair = sb("z_pair", [P, ST, 2, C])
        z_T = sb("z_T", [P, NQ, QB])
        psum = ctx.enter_context(nc.psum_tensor("psum", [P, 8, QB], F32))
        RING, Z = 4, 6

        passed = sem("passed")
        consts = sem("consts")
        shift_rows = sem("shift_rows")
        x_loaded, x_split = sem("x_loaded"), sem("x_split")
        w_loaded, w_split = sem("w_loaded"), sem("w_split")
        w_hi_done, x_hi_done = sem("w_hi_done"), sem("x_hi_done")
        proj_ready = sem("proj_ready")
        hi_ready = sem("hi_ready")
        proj_read = sem("proj_read")
        copies_ready = sem("copies_ready")
        v2_ready, v_ready = sem("v2_ready"), sem("v_ready")
        ring_ready, ring_read = sem("ring_ready"), sem("ring_read")
        neg_ready = sem("neg_ready")
        scores_ready = sem("scores_ready")
        probs_ready = sem("probs_ready")
        probs_split = sem("probs_split")
        slot_used = sem("slot_used")
        z_read = sem("z_read")
        z_done = sem("z_done")
        turned, turned_read = sem("turned"), sem("turned_read")
        z_stored = sem("z_stored")
        block = ctx.enter_context(nc.Block())

        CONSTS = 11

        def slot_views(i, n, s, *tensors):
            tiles = slot_tiles(n, s)
            if tiles[1][2] == 0:
                return [tuple(t[:, i % NP, :, :] for t in tensors)]
            return [tuple(t[:, i % NP, u, P * f:QB] for t in tensors) for u, _, f in tiles]


        @block.sync
        def _(sp):
            for started in (z_stored,):
                sp.sem_inc(started, START)
            with sp.Fori(0, B) as b:
                sp.wait_ge(x_split, b * DT + START)
                sp.dma_start(x_raw[:, :, :], xT[bass.ds(b, 1), :, :, :].rearrange("b p d s -> (b p) d s")).then_inc(x_loaded, 16)
                with sp.Fori(0, PAIRS) as p:
                    sp.wait_ge(w_split, b * PAIRS + p + START)
                    sp.dma_start(w_raw[:, :, :], wqkv[bass.ds(p, 1), :, :, :].rearrange("g p d n -> (g p) d n")).then_inc(w_loaded, 16)
                    sp.wait_ge(turned_read, (b * PAIRS + p) * NQ + NQ + START)
                    sp.dma_start(zT_dram[bass.ds(b * NQ, NQ), :, bass.ds(p, 1), :].rearrange("q p g t -> p q (g t)"),
                                 z_T[:, :, :]).then_inc(z_stored, 16)
            sp.wait_ge(z_stored, 16 * B * PAIRS + START)

        @block.gpsimd
        def _(pool):
            for started in (probs_split, v_ready, copies_ready):
                pool.sem_inc(started, START)
            nc.gpsimd.memset(ident[:, :], 0.0).then_inc(consts, 1)
            nc.gpsimd.memset(ident_b[:, :], 0.0).then_inc(consts, 1)
            nc.gpsimd.memset(mask_q[:, :], 0.0).then_inc(consts, 1)
            nc.gpsimd.memset(mask_k[:, :], 0.0).then_inc(consts, 1)
            nc.gpsimd.memset(row_sel[:, :, :], 0.0).then_inc(consts, 1)
            nc.gpsimd.memset(v3[:, :, :, 0:1], 1.0).then_inc(consts, 1)
            pool.wait_ge(consts, 6)
            for m in (ident, ident_b):
                nc.gpsimd.affine_select(out=m[:, :], in_=m[:, :], compare_op=ALU.not_equal, fill=1.0, base=0,
                                        pattern=[[-1, P]], channel_multiplier=1).then_inc(consts, 1)
            nc.gpsimd.affine_select(out=mask_q[:, :], in_=mask_q[:, :], compare_op=ALU.is_ge, fill=NEG, base=0,
                                    pattern=[[-1, P]], channel_multiplier=1).then_inc(consts, 1)
            nc.gpsimd.affine_select(out=mask_k[:, :], in_=mask_k[:, :], compare_op=ALU.is_ge, fill=NEG, base=0,
                                    pattern=[[1, P]], channel_multiplier=-1).then_inc(consts, 1)
            nc.gpsimd.affine_select(out=row_sel[:, :, :], in_=row_sel[:, :, :], compare_op=ALU.not_equal, fill=1.0,
                                    base=0, pattern=[[-1, TPB], [0, P]], channel_multiplier=1).then_inc(consts, 1)
            with pool.Fori(0, B) as b:
                with pool.Fori(0, PAIRS) as p:
                    it = b * PAIRS + p
                    pool.wait_ge(probs_split, it * NSLOT + START)
                    for g in range(QK_GROUPS):
                        mat, cols = g // NQ, slice(QB * (g % NQ), QB * (g % NQ + 1))
                        pool.wait_ge(hi_ready, it * GROUPS + g + 1)
                        for h in range(2):
                            pool.wait_ge(copies_ready, it * QK_GROUPS * 2 + 2 * g + h + START)
                            pool.sem_inc(passed, 1)
                            src, other = slice(C * h, C * h + C), slice(C - C * h, 2 * C - C * h)
                            a = (qa, ka)[mat][src, h, cols]
                            dst = qb[src, h, cols] if mat == 0 else ka[other, h, cols]
                            nc.gpsimd.tensor_scalar(dst, a.bitcast(F32), 1.0, 0.0, ALU.mult, ALU.add).then_inc(copies_ready, 1)
                    pool.wait_ge(copies_ready, (it + 1) * QK_GROUPS * 2 + START)
                    for g in range(V_GROUPS):
                        t = slice(TPB * g, TPB * g + TPB)
                        pool.wait_ge(v2_ready, it * V_GROUPS + g + 1)
                        for h in range(2):
                            last = nc.gpsimd.tensor_tensor(v3[:, t, h, 1 + 2 * C:1 + 3 * C], v_rest[:, g % 2, :, h, :],
                                                           v3[:, t, h, 1 + C:1 + 2 * C], ALU.subtract)
                        last.then_inc(v_ready, 1)
                    for i, (n, s) in enumerate(SLOTS):
                        pool.wait_ge(probs_ready, it * NSLOT + i + 1 + START)
                        for dst, full, hi in slot_views(i, n, s, p_lo, p_full, p_hi):
                            last = nc.gpsimd.tensor_tensor(dst, full, hi, ALU.subtract)
                        last.then_inc(probs_split, 1)

        @block.scalar
        def _(act):
            for started in (turned_read, probs_ready):
                act.sem_inc(started, START)
            with act.Fori(0, B) as b:
                act.wait_ge(x_loaded, b * 16 + 16)
                act.wait_ge(proj_ready, b * PAIRS * GROUPS + START)
                for d in range(DT):
                    nc.scalar.activation(x_hi[:, d, :], x_raw[:, d, :], ACT.Copy).then_inc(x_hi_done, 1)
                with act.Fori(0, PAIRS) as p:
                    it = b * PAIRS + p
                    for g in range(GROUPS):
                        act.wait_ge(proj_ready, it * GROUPS + g + 1 + START)
                        bank = psum[:, g % 4, :]
                        if g < QK_GROUPS:
                            mat, cols = g // NQ, slice(QB * (g % NQ), QB * (g % NQ + 1))
                            for h in range(2):
                                rows = slice(C * h, C * h + C)
                                last = nc.scalar.activation((qa, ka)[mat][rows, h, cols], bank[rows, :], ACT.Copy)
                        else:
                            t = slice(TPB * (g - QK_GROUPS), TPB * (g - QK_GROUPS + 1))
                            last = nc.scalar.activation(v3[:, t, :, 1:1 + C],
                                                        bank.rearrange("p (t h c) -> p t h c", t=TPB, h=2), ACT.Copy)
                        last.then_inc(hi_ready, 1)
                    for i, (n, s) in enumerate(SLOTS):
                        act.wait_ge(scores_ready, it * NSLOT + i + 1)
                        act.wait_ge(slot_used, it * NSLOT + max(0, i - NP + 1) + START)
                        banks = psum[:, 2 * (i % 2):2 * (i % 2) + 2, :]
                        tiles = slot_tiles(n, s)
                        ins = [banks] if tiles[1][2] == 0 else [banks[:, u, P * f:QB] for u, _, f in tiles]
                        for (hi, full), scores in zip(slot_views(i, n, s, p_hi, p_full), ins):
                            nc.scalar.activation(hi, scores, ACT.Exp, scale=SCALE)
                            last = nc.scalar.activation(full, scores, ACT.Exp, scale=SCALE)
                        last.then_inc(probs_ready, 1)
                    act.wait_ge(z_stored, it * 16 + START)
                    for q in range(NQ):
                        act.wait_ge(turned, it * NQ + q + 1 + START)
                        nc.scalar.activation(z_T[:, q, :], psum[:, q, :], ACT.Copy).then_inc(turned_read, 1)

        @block.vector
        def _(dve):
            for started in (x_split, w_split, proj_read, ring_read, z_done, z_read):
                dve.sem_inc(started, START)
            def ring(it, r, item):
                dve.wait_ge(ring_ready, it * RING_N + r + 1)
                bank = psum[:, RING + r % 2, :]
                n = item[1]
                if item[0] == "chunk":
                    _, n, t, c = item
                    nc.vector.reduce_max(row_max[:, n % 2, t, c:c + 1], bank[:, 0:chunk_width(n, t, c)],
                                         AX.X).then_inc(ring_read, 1)
                    if t == TPB - 1 and c == block_of(n)[1]:
                        dve.wait_ge(ring_read, it * RING_N + r + 1 + START)
                        nc.vector.tensor_reduce(neg_max[:, n % 2, :], row_max[:, n % 2, :, 0:c + 1], axis=AX.X,
                                                op=ALU.max, negate=True).then_inc(neg_ready, 1)
                else:
                    h, q = block_of(n)
                    r0 = C if h == 0 else 0
                    nc.vector.scalar_tensor_tensor(
                        out=qb[r0:r0 + TPB, h, QB * q:QB * q + QB].rearrange("r (t c) -> r t c", t=TPB),
                        in0=bank[0:TPB, 0:P].unsqueeze(1).to_broadcast([TPB, TPB, P]), scalar=SHIFT,
                        in1=row_sel[:, :, :], op0=ALU.add, op1=ALU.mult).then_inc(ring_read, 1)

            def outputs(it, n):
                dve.wait_ge(slot_used, it * NSLOT + SLOTN[n] + 1 + START)
                h, q = block_of(n)
                z = psum[:, Z:Z + 2, 0:2 * VW].rearrange("p k (t w) -> p k t w", t=2)
                dve.wait_ge(z_done, it * NBLK + n + START)
                nc.vector.reciprocal(z_rcp[:, :].rearrange("p (k t w) -> p k t w", k=2, t=2), z[:, :, :, 0:1])
                for k in range(2):
                    parts = psum[:, Z + k, 0:2 * VW].rearrange("p (t w) -> p t w", t=2)[:, :, 1:VW]
                    last = nc.vector.tensor_reduce(z_sum[:, 2 * k:2 * k + 2, :],
                                                   parts.rearrange("p t (a c) -> p t c a", a=3), axis=AX.X, op=ALU.add)
                last.then_inc(z_read, 1)
                dve.wait_ge(z_read, it * NBLK + n + 1 + START)
                dve.wait_ge(turned, it * NQ + START)
                nc.vector.tensor_tensor(z_pair[:, TPB * q:TPB * q + TPB, h, :], z_sum[:, :, :],
                                        z_rcp[:, :].unsqueeze(2).to_broadcast([P, TPB, C]), ALU.mult).then_inc(z_done, 1)

            for h, r in ((0, C), (1, 0)):
                nc.vector.memset(qb[r:r + C, h, :].bitcast(F32), 0.0).then_inc(shift_rows, 1)
                nc.vector.memset(kb[r:r + C, h, :].bitcast(F32), 0.0).then_inc(shift_rows, 1)
            dve.wait_ge(shift_rows, 4)
            for h, r in ((0, C), (1, 0)):
                nc.vector.memset(kb[r:r + TPB, h, :].bitcast(F32), 1.0).then_inc(shift_rows, 1)
            dve.wait_ge(consts, CONSTS)
            with dve.Fori(0, B) as b:
                dve.wait_ge(proj_ready, b * PAIRS * GROUPS + START)
                for d in range(DT):
                    dve.wait_ge(x_hi_done, b * DT + d + 1)
                    nc.vector.tensor_tensor(x_lo[:, d, :], x_raw[:, d, :], x_hi[:, d, :].bitcast(F32),
                                            ALU.subtract).then_inc(x_split, 1)
                with dve.Fori(0, PAIRS) as p:
                    it = b * PAIRS + p
                    dve.wait_ge(w_loaded, it * 16 + 16)
                    dve.wait_ge(proj_ready, it * GROUPS + START)
                    nc.vector.tensor_copy(w_hi[:, :, :], w_raw[:, :, :]).then_inc(w_hi_done, 1)
                    dve.wait_ge(w_hi_done, it + 1)
                    nc.vector.tensor_tensor(w_lo[:, :, :], w_raw[:, :, :], w_hi[:, :, :].bitcast(F32),
                                            ALU.subtract).then_inc(w_split, 1)
                    for g in range(GROUPS):
                        bank = psum[:, g % 4, :]
                        dve.wait_ge(hi_ready, it * GROUPS + g + 1)
                        if g < QK_GROUPS:
                            mat, cols = g // NQ, slice(QB * (g % NQ), QB * (g % NQ + 1))
                            for h in range(2):
                                src, other = slice(C * h, C * h + C), slice(C - C * h, 2 * C - C * h)
                                dst = qa[other, h, cols] if mat == 0 else kb[src, h, cols]
                                last = nc.vector.tensor_tensor(dst, bank[src, :], (qa, ka)[mat][src, h, cols].bitcast(F32),
                                                               ALU.subtract)
                            last.then_inc(proj_read, 1)
                        else:
                            k = g - QK_GROUPS
                            t = slice(TPB * k, TPB * k + TPB)
                            dve.wait_ge(v_ready, it * V_GROUPS + max(0, k - 1) + START)
                            nc.vector.tensor_tensor(v_rest[:, k % 2, :, :, :], bank.rearrange("p (t h c) -> p t h c", t=TPB, h=2),
                                                    v3[:, t, :, 1:1 + C], ALU.subtract).then_inc(proj_read, 1)
                            dve.wait_ge(proj_read, it * GROUPS + g + 1 + START)
                            nc.vector.tensor_copy(v3[:, t, :, 1 + C:1 + 2 * C], v_rest[:, k % 2, :, :, :]).then_inc(v2_ready, 1)
                    r = 0
                    for item in AHEAD:
                        ring(it, r, item)
                        r += 1
                    for i, (n, s) in enumerate(SLOTS):
                        for item in STEP_RING[i]:
                            ring(it, r, item)
                            r += 1
                        if i - LAG in SLOTN:
                            outputs(it, SLOTN.index(i - LAG))
                    outputs(it, NBLK - 1)

        @block.tensor
        def _(pe):
            for started in (turned, proj_ready, slot_used):
                pe.sem_inc(started, START)
            def project(it):
                for g in range(GROUPS):
                    if g < 4:
                        pe.wait_ge(probs_ready, it * NSLOT + START)
                        pe.wait_ge(turned_read, it * NQ + START)
                    else:
                        pe.wait_ge(proj_read, it * GROUPS + g - 3 + START)
                    if g < QK_GROUPS:
                        mat, cols = g // NQ, slice(QB * (g % NQ), QB * (g % NQ + 1))
                        w = slice(P * mat, P * mat + P)
                        terms = [(a[:, d, w], c[:, d, cols]) for d in range(DT) for a, c in ((w_hi, x_hi), (w_hi, x_lo), (w_lo, x_hi))]
                        for k, (lhsT, rhs) in enumerate(terms):
                            last = nc.tensor.matmul(psum[:, g % 4, :], lhsT, rhs, start=(k == 0), stop=(k == len(terms) - 1))
                    else:
                        for u in range(TPB):
                            t = TPB * (g - QK_GROUPS) + u
                            tok, w = slice(P * t, P * t + P), slice(2 * P, 3 * P)
                            terms = [(a[:, d, tok], c[:, d, w]) for d in range(DT) for a, c in ((x_hi, w_hi), (x_lo, w_hi), (x_hi, w_lo))]
                            for k, (lhsT, rhs) in enumerate(terms):
                                last = nc.tensor.matmul(psum[:, g % 4, P * u:P * u + P], lhsT, rhs,
                                                        start=(k == 0), stop=(k == len(terms) - 1))
                    last.then_inc(proj_ready, 1)

            def ring(it, r, item):
                pe.wait_ge(ring_read, it * RING_N + max(0, r - 1) + START)
                bank = psum[:, RING + r % 2, :]
                if item[0] == "chunk":
                    _, n, t, c = item
                    h, q = block_of(n)
                    w = chunk_width(n, t, c)
                    tile = TPB * q + t
                    diagonal = c == q
                    last = nc.tensor.matmul(bank[:, 0:w], qa[:, h, P * tile:P * tile + P], ka[:, h, QB * c:QB * c + w],
                                            start=True, stop=not diagonal)
                    if diagonal:
                        last = nc.tensor.matmul(bank[:, w - P:w], ident_b[:, :], mask_q[:, :], start=False, stop=True)
                else:
                    n = item[1]
                    pe.wait_ge(neg_ready, it * NBLK + n + 1)
                    last = nc.tensor.transpose(bank[0:TPB, 0:P], neg_max[:, n % 2, :], ident[:, :])
                last.then_inc(ring_ready, 1)

            def scores(it, i):
                n, s = SLOTS[i]
                h, q = block_of(n)
                pe.wait_ge(probs_ready, it * NSLOT + max(0, i - 1) + START)
                tiles = slot_tiles(n, s)
                for u, k, f in tiles:
                    cols = slice(QB * q + P * f, QB * q + QB)
                    nc.tensor.matmul(psum[:, 2 * (i % 2) + u, P * f:QB], ka[:, h, P * k:P * k + P], qa[:, h, cols],
                                     start=True, stop=False)
                    if s == 0 and u == 0:
                        pe.wait_ge(ring_read, it * RING_N + TURN_AT[n] + 1 + START)
                    last = nc.tensor.matmul(psum[:, 2 * (i % 2) + u, P * f:QB], kb[:, h, P * k:P * k + P], qb[:, h, cols],
                                            start=False, stop=k < TPB * q)
                    if k >= TPB * q:
                        last = nc.tensor.matmul(psum[:, 2 * (i % 2) + u, P * f:P * f + P], ident_b[:, :], mask_k[:, :],
                                                start=False, stop=True)
                last.then_inc(scores_ready, 1)

            def products(it, i):
                n, s = SLOTS[i]
                h, q = block_of(n)
                pe.wait_ge(probs_split, it * NSLOT + i + 1 + START)
                if s == 0:
                    pe.wait_ge(z_read, it * NBLK + n + START)
                for u, k, f in slot_tiles(n, s):
                    for t in range(f, TPB):
                        z = psum[:, Z + t // 2, VW * (t % 2):VW * (t % 2) + VW]
                        cols = slice(P * t, P * t + P)
                        nc.tensor.matmul(z, p_hi[:, i % NP, u, cols], v3[:, k, h, 0:VW], start=(k == 0 and t % 2 == 0),
                                         stop=False, skip_group_check=True)
                        last = nc.tensor.matmul(z[:, 0:VW - C], p_lo[:, i % NP, u, cols], v3[:, k, h, 0:VW - C],
                                                start=False, stop=(k == TPB * q + t), skip_group_check=True)
                last.then_inc(slot_used, 1)

            pe.wait_ge(consts, CONSTS)
            pe.wait_ge(shift_rows, 6)
            with pe.Fori(0, B) as b:
                with pe.Fori(0, PAIRS) as p:
                    it = b * PAIRS + p
                    pe.wait_ge(x_split, b * DT + DT + START)
                    pe.wait_ge(w_split, it + 1 + START)
                    project(it)
                    pe.wait_ge(proj_read, it * GROUPS + GROUPS + START)
                    pe.wait_ge(copies_ready, (it + 1) * QK_GROUPS * 2 + START)
                    pe.wait_ge(v_ready, it * V_GROUPS + V_GROUPS + START)
                    r = 0
                    for item in AHEAD:
                        ring(it, r, item)
                        r += 1
                    for i in range(NSLOT):
                        scores(it, i)
                        for item in STEP_RING[i]:
                            ring(it, r, item)
                            r += 1
                        if i >= LAG:
                            products(it, i - LAG)
                    for i in range(NSLOT - LAG, NSLOT):
                        products(it, i)
                    pe.wait_ge(probs_ready, it * NSLOT + NSLOT + START)
                    pe.wait_ge(z_done, it * NBLK + NBLK + START)
                    for q in range(NQ):
                        for u in range(TPB):
                            t = TPB * q + u
                            last = nc.tensor.transpose(psum[:, q, P * u:P * u + P],
                                                       z_pair[:, t, :, :].rearrange("p h c -> p (h c)"), ident[:, :])
                        last.then_inc(turned, 1)


TURN_AT = [([*AHEAD, *(x for step in STEP_RING for x in step)]).index(("turn", n)) for n in range(NBLK)]


def feed_forward(nc, x, zT_dram, wout, b_out, gamma, beta, q1, s1, b1, q2, s2, b2, out):
    with ExitStack() as ctx:
        def sb(name, shape, dt=F32):
            return ctx.enter_context(nc.sbuf_tensor(name, shape, dt))

        def sem(name):
            return ctx.enter_context(nc.semaphore(name))

        identF = sb("identF", [P, P])
        wo = sb("wo", [P, PAIRS, D])
        w1 = sb("w1", [P, DT, F])
        w2 = sb("w2", [P, FT, D])
        q1s, q2s = sb("q1s", [P, DT, F], I32), sb("q2s", [P, FT, D], I32)
        s1s, s2s = sb("s1s", [P, DT, F]), sb("s2s", [P, FT, D])
        bo_s, b2_s, hb2 = sb("bo_s", [P, D]), sb("b2_s", [P, D]), sb("hb2", [P, D])
        gam, bet, b1_s = sb("gam", [P, DT]), sb("bet", [P, DT]), sb("b1_s", [P, FT])
        zT = sb("zT", [P, 2, PAIRS, QB])
        xs = sb("xs", [P, 2, TPB, D])
        y = sb("y", [P, TPB, D])
        ya = sb("ya", [P, TPB, D])
        x1 = sb("x1", [P, TPB, D])
        xn = sb("xn", [P, TPB, D])
        base = sb("base", [P, 2, TPB, D])
        hT = sb("hT", [P, DT, QB])
        aT = sb("aT", [P, FT, QB])
        o = sb("o", [P, TPB, D])
        res = sb("res", [P, 2, TPB, D])
        stats, mv, var_e, std, rstd = (sb(n, s) for n, s in (("stats", [P, TPB, 6]), ("mv", [P, TPB, 2]),
                                                             ("var_e", [P, TPB]), ("std", [P, TPB]), ("rstd", [P, TPB])))
        psum = ctx.enter_context(nc.psum_tensor("psum2", [P, 8, QB], F32))
        WO, HT, FC, ZO = 0, 2, 4, 6

        passed = sem("passed")
        w_in, idF = sem("w_in"), sem("idF")
        zx_in = [sem("zx_in0"), sem("zx_in1")]
        wo_ready, wo_read = sem("wo_ready"), sem("wo_read")
        first_norms, last_norm = sem("first_norms"), sem("last_norm")
        weights = sem("weights")
        norm_ready, hT_ps, hT_ready = sem("norm_ready"), sem("hT_ps"), sem("hT_ready")
        var_ready, std_ready = sem("var_ready"), sem("std_ready")
        fc1_ready, act_ready = sem("fc1_ready"), sem("act_ready")
        fc2_ready, fc2_read = sem("fc2_ready"), sem("fc2_read")
        res_ready = sem("res_ready")
        stored = [sem("stored0"), sem("stored1")]
        block = ctx.enter_context(nc.Block())

        x_blk = x.rearrange("b (q t p) d -> (b q) p t d", t=TPB, p=P)
        out_blk = out.rearrange("b (q t p) d -> (b q) p t d", t=TPB, p=P)

        @block.sync
        def _(sp):
            for started in (stored[0], stored[1]):
                sp.sem_inc(started, START)
            def load(i, k):
                sp.dma_start(zT[:, k, :, :], zT_dram[bass.ds(i, 1), :, :, :].rearrange("i p g t -> (i p) g t")).then_inc(zx_in[k], 16)
                sp.dma_start(xs[:, k, :, :], x_blk[bass.ds(i, 1), :, :, :].rearrange("i p t d -> (i p) t d")).then_inc(zx_in[k], 16)
            load(0, 0)
            sp.dma_start(wo[:, :, :], wout).then_inc(w_in, 16)
            load(1, 1)
            sp.dma_start(q1s[:, :, :], q1.rearrange("(k p) f -> p k f", p=P)).then_inc(w_in, 16)
            sp.dma_start(q2s[:, :, :], q2.rearrange("(k p) f -> p k f", p=P)).then_inc(w_in, 16)
            for k in range(DT):
                sp.dma_start(s1s[:, k, :], s1[k:k + 1, :].to_broadcast([P, F])).then_inc(w_in, 16)
            for k in range(FT):
                sp.dma_start(s2s[:, k, :], s2[k:k + 1, :].to_broadcast([P, D])).then_inc(w_in, 16)
            sp.dma_start(bo_s[:, :], b_out.unsqueeze(0).to_broadcast([P, D])).then_inc(w_in, 16)
            sp.dma_start(b2_s[:, :], b2.unsqueeze(0).to_broadcast([P, D])).then_inc(w_in, 16)
            sp.dma_start(gam[:, :], gamma).then_inc(w_in, 16)
            sp.dma_start(bet[:, :], beta).then_inc(w_in, 16)
            sp.dma_start(b1_s[:, :], b1).then_inc(w_in, 16)
            def store(i, k):
                sp.wait_ge(res_ready, i + 1)
                sp.dma_start(out_blk[bass.ds(i, 1), :, :, :].rearrange("i p t d -> (i p) t d"),
                             res[:, k, :, :]).then_inc(stored[k], 16)
            with sp.Fori(0, TOKB // 2 - 1) as j:
                for k in range(2):
                    store(2 * j + k, k)
                    load(2 * j + k + 2, k)
            for k in range(2):
                store(TOKB - 2 + k, k)
            for k in range(2):
                sp.wait_ge(stored[k], 16 * (TOKB // 2) + START)
        W_IN = 16 * (3 + DT + FT + 5)

        @block.gpsimd
        def _(pool):
            nc.gpsimd.memset(identF[:, :], 0.0).then_inc(idF, 1)
            pool.wait_ge(idF, 1)
            nc.gpsimd.affine_select(out=identF[:, :], in_=identF[:, :], compare_op=ALU.not_equal, fill=1.0, base=0,
                                    pattern=[[-1, P]], channel_multiplier=1).then_inc(idF, 1)

        def over_blocks(eng, step):
            with eng.Fori(0, TOKB // 2 - 1) as j:
                for k in range(2):
                    step(2 * j + k, k, True)
            step(TOKB - 2, 0, True)
            step(TOKB - 1, 1, False)

        @block.tensor
        def _(pe):
            for started in (hT_ps, fc1_ready, fc2_ready):
                pe.sem_inc(started, START)
            def out_projection(i, k):
                pe.wait_ge(zx_in[k], 32 * ((i - k) // 2 + 1) if isinstance(i, int) else (i - k) * 16 + 32)
                pe.wait_ge(wo_read, i + START)
                for t in range(TPB):
                    for g in range(PAIRS):
                        last = nc.tensor.matmul(psum[:, WO + t // 2, D * (t % 2):D * (t % 2) + D],
                                                zT[:, k, g, P * t:P * t + P], wo[:, g, :], start=(g == 0), stop=(g == PAIRS - 1))
                last.then_inc(wo_ready, 1)

            def step(i, k, more):
                pe.wait_ge(norm_ready, i + 1)
                pe.wait_ge(hT_ready, i + START)
                for d in range(DT):
                    for t in range(TPB):
                        last = nc.tensor.transpose(psum[:, HT + d, P * t:P * t + P], xn[:, t, P * d:P * d + P], identF[:, :])
                last.then_inc(hT_ps, 1)
                pe.wait_ge(hT_ready, i + 1 + START)
                for f in range(FT):
                    pe.wait_ge(act_ready, i * FT + max(0, f - 1) + START)
                    for d in range(DT):
                        last = nc.tensor.matmul(psum[:, FC + f % 2, :], w1[:, d, P * f:P * f + P], hT[:, d, :],
                                                start=(d == 0), stop=(d == DT - 1))
                    last.then_inc(fc1_ready, 1)
                if more:
                    out_projection(i + 1, 1 - k)
                pe.wait_ge(act_ready, i * FT + FT + START)
                pe.wait_ge(fc2_read, i + START)
                for t in range(TPB):
                    for f in range(FT):
                        last = nc.tensor.matmul(psum[:, ZO + t // 2, D * (t % 2):D * (t % 2) + D],
                                                aT[:, f, P * t:P * t + P], w2[:, f, :], start=(f == 0), stop=(f == FT - 1))
                last.then_inc(fc2_ready, 1)

            pe.wait_ge(w_in, W_IN)
            pe.wait_ge(idF, 2)
            out_projection(0, 0)
            pe.wait_ge(weights, 2)
            over_blocks(pe, step)

        @block.scalar
        def _(act):
            for started in (act_ready,):
                act.sem_inc(started, START)
            def root(n):
                act.wait_ge(var_ready, n + 1)
                nc.scalar.activation(std[:, :], var_e[:, :], ACT.Sqrt).then_inc(std_ready, 1)

            def step(i, k, more):
                for f in range(FT):
                    act.wait_ge(fc1_ready, i * FT + f + 1 + START)
                    act.wait_ge(fc2_ready, i + START)
                    nc.scalar.activation(aT[:, f, :], psum[:, FC + f % 2, :], ACT.Silu, bias=b1_s[:, f:f + 1]).then_inc(act_ready, 1)
                if more:
                    root(3 * i + 2)
                    root(3 * i + 3)
                    root(3 * i + 4)
                else:
                    root(3 * i + 2)

            act.wait_ge(w_in, W_IN)
            root(0)
            root(1)
            over_blocks(act, step)

        @block.vector
        def _(dve):
            for started in (wo_read, fc2_read, hT_ready):
                dve.sem_inc(started, START)
            class Chain:
                def __init__(self, sem, at):
                    self.sem, self.at = sem, at

                def done(self, instruction):
                    self.at = self.at + 1
                    instruction.then_inc(self.sem, 1)
                    dve.wait_ge(self.sem, self.at)

            def normalise(chain, src, dst, n):
                for t in range(TPB):
                    last = nc.vector.bn_stats(stats[:, t, :], src[:, t, :])
                chain.done(last)
                dve.sem_inc(passed, 1)
                for t in range(TPB):
                    last = nc.vector.bn_aggr(mv[:, t, :], stats[:, t, :])
                chain.done(last)
                nc.vector.tensor_scalar(var_e[:, :], mv[:, :, 1], EPS, None, ALU.add).then_inc(var_ready, 1)
                dve.wait_ge(std_ready, n + 1)
                chain.done(nc.vector.reciprocal(rstd[:, :], std[:, :]))
                for t in range(TPB):
                    last = nc.vector.tensor_scalar(dst[:, t, :], src[:, t, :], mv[:, t, 0:1], rstd[:, t:t + 1],
                                                   ALU.subtract, ALU.mult)
                return last

            NORMS, LAST = 9, 3

            def to_norms(i, k, n):
                chain = Chain(first_norms, i * NORMS)
                dve.wait_ge(wo_ready, i + 1)
                sums = psum[:, WO:WO + 2, :].rearrange("p k (t d) -> p (k t) d", t=2)
                nc.vector.tensor_tensor(y[:, :, :], sums, xs[:, k, :, :], ALU.add).then_inc(wo_read, 1)
                dve.wait_ge(wo_read, i + 1 + START)
                chain.done(nc.vector.tensor_tensor(ya[:, :, :], y[:, :, :], bo_s[:, :].unsqueeze(1).to_broadcast([P, TPB, D]), ALU.add))
                chain.done(normalise(chain, ya, x1, n))
                dve.wait_ge(hT_ps, i + START)
                last = normalise(chain, x1, xn, n + 1)
                last.then_inc(norm_ready, 1)
                nc.vector.scalar_tensor_tensor(out=base[:, k, :, :], in0=x1[:, :, :], scalar=2.0,
                                               in1=hb2[:, :].unsqueeze(1).to_broadcast([P, TPB, D]),
                                               op0=ALU.mult, op1=ALU.add).then_inc(first_norms, 1)
                assert isinstance(i, int) is False or chain.at + 1 == i * NORMS + NORMS, chain.at

            def step(i, k, more):
                dve.wait_ge(hT_ps, i + 1 + START)
                dve.wait_ge(fc1_ready, i * FT + START)
                for d in range(DT):
                    last = nc.vector.tensor_scalar(hT[:, d, :], psum[:, HT + d, :], gam[:, d:d + 1], bet[:, d:d + 1],
                                                   ALU.mult, ALU.add)
                last.then_inc(hT_ready, 1)
                if more:
                    to_norms(i + 1, 1 - k, 3 * i + 2)
                chain = Chain(last_norm, i * LAST)
                dve.wait_ge(fc2_ready, i + 1 + START)
                dve.wait_ge(first_norms, i * NORMS + NORMS)
                sums = psum[:, ZO:ZO + 2, :].rearrange("p k (t d) -> p (k t) d", t=2)
                nc.vector.scalar_tensor_tensor(out=o[:, :, :], in0=sums, scalar=0.5, in1=base[:, k, :, :],
                                               op0=ALU.mult, op1=ALU.add).then_inc(fc2_read, 1)
                dve.wait_ge(fc2_read, i + 1 + START)
                dve.wait_ge(stored[k], (((i - k) // 2) * 16 if isinstance(i, int) else (i - k) * 8) + START)
                last = normalise(chain, o, res[:, k, :, :], 3 * i + 4 if more else 3 * i + 2)
                last.then_inc(res_ready, 1)

            dve.wait_ge(w_in, W_IN)
            nc.vector.scalar_tensor_tensor(out=w1[:, :, :], in0=q1s[:, :, :], scalar=-128.0, in1=s1s[:, :, :],
                                           op0=ALU.add, op1=ALU.mult).then_inc(weights, 1)
            nc.vector.scalar_tensor_tensor(out=w2[:, :, :], in0=q2s[:, :, :], scalar=-128.0, in1=s2s[:, :, :],
                                           op0=ALU.add, op1=ALU.mult).then_inc(weights, 1)
            nc.vector.tensor_scalar(hb2[:, :], b2_s[:, :], 0.5, None, ALU.mult).then_inc(weights, 1)
            dve.wait_ge(weights, 3)
            to_norms(0, 0, 0)
            over_blocks(dve, step)


def build(nc, x, xT, wqkv, wout, b_out, gamma, beta, q1, s1, b1, q2, s2, b2, out):
    zT_dram = nc.dram_tensor("zT_dram", [TOKB, P, PAIRS, QB], F32, kind="Internal").ap()
    attention(nc, xT, wqkv, zT_dram)
    feed_forward(nc, x, zT_dram, wout, b_out, gamma, beta, q1, s1, b1, q2, s2, b2, out)


def kernel(**inputs):
    import numpy as np
    import concourse.bacc as bacc
    from concourse.bass_utils import run_bass_kernel_spmd as run

    a = {n.removeprefix("L0_"): np.asarray(v) for n, v in inputs.items()}
    x = a["attn_resid"]
    xT = x.reshape(B, S, DT, P).transpose(0, 3, 2, 1)
    w = np.stack([a["attn_W_Q"], a["attn_W_K"], a["attn_W_V"]]).reshape(3, DT, P, PAIRS, 2 * C)
    wqkv = w.transpose(3, 2, 1, 0, 4).reshape(PAIRS, P, DT, 3 * P)
    wout = a["attn_W_out"].reshape(C, PAIRS, 2, D).transpose(2, 0, 1, 3).reshape(P, PAIRS, D)
    arrays = {
        "x": x, "xT": xT, "wqkv": wqkv, "wout": wout, "b_out": a["attn_b_out"],
        "gamma": a["ffn_ln_gamma"].reshape(DT, P).T, "beta": a["ffn_ln_beta"].reshape(DT, P).T,
        "q1": a["ffn_fc1_q"], "s1": a["ffn_fc1_scales"], "b1": a["ffn_fc1_bias"].reshape(FT, P).T,
        "q2": a["ffn_fc2_q"], "s2": a["ffn_fc2_scales"], "b2": a["ffn_fc2_bias"],
    }
    arrays = {f"{n}_dram": np.ascontiguousarray(v) for n, v in arrays.items()}
    nc = bacc.Bacc("TRN2", target_bir_lowering=False, num_devices=1)
    d = {n.removesuffix("_dram"): nc.dram_tensor(n, v.shape, mybir.dt.from_np(v.dtype), kind="ExternalInput").ap()
         for n, v in arrays.items()}
    out = nc.dram_tensor("out_dram", (B, S, D), F32, kind="ExternalOutput").ap()
    build(nc, out=out, **d)
    r = run(nc, [arrays], core_ids=[0])
    return r.results[0]["out_dram"]
```

```python
from contextlib import ExitStack

import concourse.bass as bass
from concourse import mybir

F32 = mybir.dt.float32
F32R = mybir.dt.float32r
BF16 = mybir.dt.bfloat16
F16 = mybir.dt.float16
I32 = mybir.dt.int32
ALU = mybir.AluOpType
ACT = mybir.ActivationFunctionType
AX = mybir.AxisListType

P = 128
B, S, D = 2, 2048, 256
H, C = 16, 64
F, G = 1024, 128
DT = D // P
FT = F // P
PAIRS = H // 2
ST = S // P
QB = 512
NQ = S // QB
NBLK = 2 * NQ
TPB = QB // P
VW = 3 * C + 1
VS = VW + 1
START = 1
LAG = 3
NP = 5
NEG = -1.0e30
EPS = 1e-5
SCALE = C ** -0.5
SHIFT = 5.545177444479562 / SCALE
TOKB = B * NQ


Q_ORDER = [1, 3, 2, 0]


def block_of(n):
    return n % 2, Q_ORDER[n // 2]


SLOTS = [(n, s) for n in range(NBLK) for s in range(2 * (block_of(n)[1] + 1))]
SLOT0 = [min(i for i, (m, _) in enumerate(SLOTS) if m == n) for n in range(NBLK)]
SLOTN = [max(i for i, (m, _) in enumerate(SLOTS) if m == n) for n in range(NBLK)]
NSLOT = len(SLOTS)


def chunks_of(n):
    q = block_of(n)[1]
    return [("chunk", n, t, c) for t in range(TPB) for c in range(q + 1)]


def chunk_width(n, t, c):
    return QB if c < block_of(n)[1] else P * (t + 1)


def slot_tiles(n, s):
    q = block_of(n)[1]
    return [(i, 2 * s + i, max(0, 2 * s + i - TPB * q)) for i in range(2)]


X_STEPS, W_STEP = [5, 11, 17, 23], 28


def ring_schedule(more):
    ahead = chunks_of(0) + [("turn", 0)]
    steps = [[] for _ in SLOTS]
    for n in range(1, NBLK):
        first, last = SLOT0[n - 1], SLOTN[n - 1]
        widths = [chunk_width(*x[1:]) for x in chunks_of(n)]
        tiles = [sum(TPB - f for _, _, f in slot_tiles(*SLOTS[i])) for i in range(first, last)]
        i, done = 0, 0
        for x, w in zip(chunks_of(n), widths):
            while done + w / 2 > sum(widths) * sum(tiles[:i + 1]) / sum(tiles):
                i += 1
            steps[first + i].append(x)
            done += w
        steps[last].append(("turn", n))
    if more:
        for u, i in enumerate(X_STEPS):
            steps[i].append(("values", u))
    r, placed = len(ahead), []
    for step in steps:
        placed.append([(r + j, x) for j, x in enumerate(step)])
        r += len(step)
    return list(enumerate(ahead)), placed, r


AHEAD, _, RING_N = ring_schedule(True)
STEP_RING = {more: ring_schedule(more)[1] for more in (True, False)}
TURN_AT = {more: {x[1]: r for r, x in AHEAD + sum(STEP_RING[more], []) if x[0] == "turn"} for more in (True, False)}
RING_0 = NQ
GROUP_LIST = [("q", 1), ("k", 0), ("k", 1), ("k", 2), ("k", 3), ("q", 3), ("q", 2), ("q", 0)]
GROUPS = len(GROUP_LIST)
FIRST_GROUPS = 3
TAIL = NSLOT - LAG


def step_work(i, more):
    places = STEP_RING[more][i]
    work = [("scores", i, 0), ("scores", i, 1)] + ([("products", i - LAG, 0), ("products", i - LAG, 1)] if i >= LAG else [])
    order = []
    for k, x in enumerate(work):
        order.append(x)
        if x[0] == "products" and x[2] == 1 and x[1] in SLOTN:
            order.append(("outputs", SLOTN.index(x[1])))
        order += [("ring", *y) for y in places[len(places) * k // len(work):len(places) * (k + 1) // len(work)]]
    return order


def between_pairs():
    order = []
    products = {1: TAIL, 2: TAIL + 1, 3: TAIL + 2}
    ahead = AHEAD
    for g in range(GROUPS):
        order.append(("group", g))
        if g in products:
            i = products[g]
            order.append(("products", i))
            order += [("outputs", n) for n in range(NBLK) if SLOTN[n] == i]
            if i == NSLOT - 1:
                order.append(("values",))
        if g >= FIRST_GROUPS:
            take = -(-len(ahead) // (GROUPS - g))
            order += [("ring", *x) for x in ahead[:take]]
            ahead = ahead[take:]
    return order + [("turned", q) for q in range(NQ)]


BETWEEN = between_pairs()



def attention(nc, xT, wqkv, zT_dram):
    with ExitStack() as ctx:
        def sb(name, shape, dt=F32):
            return ctx.enter_context(nc.sbuf_tensor(name, shape, dt))

        def sem(name):
            return ctx.enter_context(nc.semaphore(name))

        ident = sb("ident", [P, P])
        ident_b = sb("ident_b", [P, P], BF16)
        mask_q = sb("mask_q", [P, P], BF16)
        mask_k = sb("mask_k", [P, P], BF16)
        row_sel = sb("row_sel", [TPB, TPB, P])
        qa = sb("qa", [P, 2, S], F32R)
        qb = sb("qb", [P, 2, S], F32R)
        ka = sb("ka", [P, 2, S], F32R)
        kb = sb("kb", [P, 2, S], F32R)
        x_raw = sb("x_raw", [P, 2, DT, QB])
        x_hi = sb("x_hi", [P, DT, S], F32R)
        x_lo = sb("x_lo", [P, DT, S], F32R)
        w_raw = sb("w_raw", [P, DT, 3 * P])
        w_hi = sb("w_hi", [P, DT, 2 * P], F32R)
        w_lo = sb("w_lo", [P, DT, 2 * P], F32R)
        v3 = sb("v3", [P, ST, 2, VS], BF16)
        v_next = sb("v_next", [P, ST, 2, VS], BF16)
        v_rest = sb("v_rest", [P, 2, TPB, 2, C])
        p_full = sb("p_full", [P, NP, 2, QB])
        p_hi = sb("p_hi", [P, NP, 2, QB], F16)
        p_lo = sb("p_lo", [P, NP, 2, QB], F16)
        row_max = sb("row_max", [P, 2, TPB, NQ])
        neg_max = sb("neg_max", [P, 2, TPB])
        z_rcp = sb("z_rcp", [P, TPB])
        z_sum = sb("z_sum", [P, TPB, C])
        z_pair = sb("z_pair", [P, ST, 2, C])
        z_T = sb("z_T", [P, NQ, QB])
        psum = ctx.enter_context(nc.psum_tensor("psum", [P, 8, QB], F32))
        RING, Z = 4, 6

        passed = sem("passed")
        consts = sem("consts")
        shift_rows = sem("shift_rows")
        x_loaded, x_split = [sem("x_loaded0"), sem("x_loaded1")], sem("x_split")
        w_loaded, w_split = sem("w_loaded"), sem("w_split")
        w_hi_done, x_hi_done = sem("w_hi_done"), sem("x_hi_done")
        proj_ready = sem("proj_ready")
        hi_ready = sem("hi_ready")
        proj_read = sem("proj_read")
        copies_ready = sem("copies_ready")
        v1_ready, v2_ready, v_ready = sem("v1_ready"), sem("v2_ready"), sem("v_ready")
        v_copied = sem("v_copied")
        ring_ready, ring_read = sem("ring_ready"), sem("ring_read")
        neg_ready = sem("neg_ready")
        scores_ready = sem("scores_ready")
        probs_ready = sem("probs_ready")
        probs_split = sem("probs_split")
        slot_used = sem("slot_used")
        z_read = sem("z_read")
        z_done = sem("z_done")
        turned, turned_read = sem("turned"), sem("turned_read")
        z_stored = sem("z_stored")
        block = ctx.enter_context(nc.Block())

        CONSTS = 12

        def over_pairs(eng, pair):
            with eng.Fori(0, B * PAIRS - 1) as it:
                pair(it, True)
            pair(B * PAIRS - 1, False)

        def slot_views(i, n, s, *tensors):
            tiles = slot_tiles(n, s)
            if tiles[1][2] == 0:
                return [tuple(t[:, i % NP, :, :] for t in tensors)]
            return [tuple(t[:, i % NP, u, P * f:QB] for t in tensors) for u, _, f in tiles]


        @block.sync
        def _(sp):
            for started in (z_stored,):
                sp.sem_inc(started, START)

            def load(m):
                sp.wait_ge(w_split, m + START)
                sp.wait_ge(v1_ready, m * NQ + START)
                sp.dma_start(w_raw[:, :, :], wqkv[bass.ds(m % PAIRS, 1), :, :, :].rearrange("g p d n -> (g p) d n")).then_inc(w_loaded, 16)
                for u in range(NQ):
                    sp.wait_ge(x_split, m * NQ + max(0, u - 1) + START)
                    sp.wait_ge(v1_ready, m * NQ + max(0, u - 1) + START)
                    sp.dma_start(x_raw[:, u % 2, :, :],
                                 xT[bass.ds(m // PAIRS, 1), :, :, QB * u:QB * u + QB].rearrange("b p d s -> (b p) d s")
                                 ).then_inc(x_loaded[u % 2], 16)

            def store(m):
                sp.wait_ge(turned_read, m * NQ + NQ + START)
                sp.dma_start(zT_dram[bass.ds((m // PAIRS) * NQ, NQ), :, bass.ds(m % PAIRS, 1), :].rearrange("q p g t -> p q (g t)"),
                             z_T[:, :, :]).then_inc(z_stored, 16)

            load(0)
            with sp.Fori(0, B * PAIRS - 1) as it:
                load(it + 1)
                store(it)
            store(B * PAIRS - 1)
            sp.wait_ge(z_stored, 16 * B * PAIRS + START)

        @block.gpsimd
        def _(pool):
            for started in (probs_split, v_ready, copies_ready):
                pool.sem_inc(started, START)
            nc.gpsimd.memset(ident[:, :], 0.0).then_inc(consts, 1)
            nc.gpsimd.memset(ident_b[:, :], 0.0).then_inc(consts, 1)
            nc.gpsimd.memset(mask_q[:, :], 0.0).then_inc(consts, 1)
            nc.gpsimd.memset(mask_k[:, :], 0.0).then_inc(consts, 1)
            nc.gpsimd.memset(row_sel[:, :, :], 0.0).then_inc(consts, 1)
            nc.gpsimd.memset(v_next[:, :, :, 0:1], 1.0).then_inc(consts, 1)
            nc.gpsimd.memset(v_next[:, :, :, VW:VS], 0.0).then_inc(consts, 1)
            pool.wait_ge(consts, 7)
            for m in (ident, ident_b):
                nc.gpsimd.affine_select(out=m[:, :], in_=m[:, :], compare_op=ALU.not_equal, fill=1.0, base=0,
                                        pattern=[[-1, P]], channel_multiplier=1).then_inc(consts, 1)
            nc.gpsimd.affine_select(out=mask_q[:, :], in_=mask_q[:, :], compare_op=ALU.is_ge, fill=NEG, base=0,
                                    pattern=[[-1, P]], channel_multiplier=1).then_inc(consts, 1)
            nc.gpsimd.affine_select(out=mask_k[:, :], in_=mask_k[:, :], compare_op=ALU.is_ge, fill=NEG, base=0,
                                    pattern=[[1, P]], channel_multiplier=-1).then_inc(consts, 1)
            nc.gpsimd.affine_select(out=row_sel[:, :, :], in_=row_sel[:, :, :], compare_op=ALU.not_equal, fill=1.0,
                                    base=0, pattern=[[-1, TPB], [0, P]], channel_multiplier=1).then_inc(consts, 1)

            def values(m, u):
                t = slice(TPB * u, TPB * u + TPB)
                pool.wait_ge(v2_ready, m * NQ + u + 1)
                for h in range(2):
                    last = nc.gpsimd.tensor_tensor(v_next[:, t, h, 1 + 2 * C:1 + 3 * C], v_rest[:, u % 2, :, h, :],
                                                   v_next[:, t, h, 1 + C:1 + 2 * C], ALU.subtract)
                last.then_inc(v_ready, 1)

            def group(m, g):
                kind, u = GROUP_LIST[g]
                cols = slice(QB * u, QB * u + QB)
                pool.wait_ge(hi_ready, m * GROUPS + g + 1)
                for h in range(2):
                    src, other = slice(C * h, C * h + C), slice(C - C * h, 2 * C - C * h)
                    a = (qa if kind == "q" else ka)[src, h, cols]
                    dst = qb[src, h, cols] if kind == "q" else ka[other, h, cols]
                    pool.wait_ge(copies_ready, m * GROUPS * 2 + 2 * g + h + START)
                    pool.sem_inc(passed, 1)
                    nc.gpsimd.tensor_scalar(dst, a.bitcast(F32), 1.0, 0.0, ALU.mult, ALU.add).then_inc(copies_ready, 1)
                if g == GROUPS - 1:
                    pool.wait_ge(copies_ready, (m + 1) * GROUPS * 2 + START)

            def pair(it, more):
                for i, (n, s) in enumerate(SLOTS):
                    pool.wait_ge(probs_ready, it * NSLOT + i + 1 + START)
                    for dst, full, hi in slot_views(i, n, s, p_lo, p_full, p_hi):
                        last = nc.gpsimd.tensor_tensor(dst, full, hi, ALU.subtract)
                    last.then_inc(probs_split, 1)
                    if more and i - 1 in X_STEPS:
                        values(it + 1, X_STEPS.index(i - 1))
                if more:
                    pool.wait_ge(probs_split, it * NSLOT + NSLOT + START)
                    for g in range(GROUPS):
                        group(it + 1, g)

            for u in range(NQ):
                values(0, u)
            pool.wait_ge(v_ready, NQ + START)
            for g in range(GROUPS):
                group(0, g)
            over_pairs(pool, pair)

        @block.scalar
        def _(act):
            for started in (turned_read, probs_ready):
                act.sem_inc(started, START)

            def split_x(m, u):
                act.wait_ge(x_loaded[u % 2], m * 32 + 16 * (u // 2) + 16)
                act.wait_ge(proj_ready, m * GROUPS + START)
                nc.scalar.activation(x_hi[:, :, QB * u:QB * u + QB], x_raw[:, u % 2, :, :], ACT.Copy).then_inc(x_hi_done, 1)

            def group(m, g):
                kind, u = GROUP_LIST[g]
                act.wait_ge(proj_ready, m * GROUPS + g + 1 + START)
                bank = psum[:, g % 4, :]
                for h in range(2):
                    rows = slice(C * h, C * h + C)
                    last = nc.scalar.activation((qa if kind == "q" else ka)[rows, h, QB * u:QB * u + QB], bank[rows, :], ACT.Copy)
                last.then_inc(hi_ready, 1)

            def pair(it, more):
                for i, (n, s) in enumerate(SLOTS):
                    act.wait_ge(scores_ready, it * NSLOT + i + 1)
                    act.wait_ge(slot_used, it * NSLOT + max(0, i - NP + 1) + START)
                    banks = psum[:, 2 * (i % 2):2 * (i % 2) + 2, :]
                    tiles = slot_tiles(n, s)
                    ins = [banks] if tiles[1][2] == 0 else [banks[:, u, P * f:QB] for u, _, f in tiles]
                    for (hi, full), scores in zip(slot_views(i, n, s, p_hi, p_full), ins):
                        nc.scalar.activation(hi, scores, ACT.Exp, scale=SCALE)
                        last = nc.scalar.activation(full, scores, ACT.Exp, scale=SCALE)
                    last.then_inc(probs_ready, 1)
                    if more and i in X_STEPS:
                        split_x(it + 1, X_STEPS.index(i))
                if more:
                    for g in range(GROUPS):
                        group(it + 1, g)
                act.wait_ge(z_stored, it * 16 + START)
                for q in range(NQ):
                    act.wait_ge(turned, it * NQ + q + 1 + START)
                    nc.scalar.activation(z_T[:, q, :], psum[:, q, :], ACT.Copy).then_inc(turned_read, 1)

            for u in range(NQ):
                split_x(0, u)
            for g in range(GROUPS):
                group(0, g)
            over_pairs(act, pair)

        @block.vector
        def _(dve):
            for started in (x_split, w_split, proj_read, ring_read, z_done, z_read, v1_ready, v_copied):
                dve.sem_inc(started, START)
            def ring(before, m, r, item):
                dve.wait_ge(ring_ready, before + r + 1)
                bank = psum[:, RING + r % 2, :]
                n = item[1]
                if item[0] == "values":
                    u, k = item[1], item[1] % 2
                    t = slice(TPB * u, TPB * u + TPB)
                    v = bank.rearrange("p (t h c) -> p t h c", t=TPB, h=2)
                    nc.vector.tensor_copy(v_next[:, t, :, 1:1 + C], v).then_inc(v1_ready, 1)
                    dve.wait_ge(v_ready, m * NQ + max(0, u - 1) + START)
                    dve.wait_ge(v1_ready, m * NQ + u + 1 + START)
                    nc.vector.tensor_tensor(v_rest[:, k, :, :, :], v,
                                            v_next[:, t, :, 1:1 + C], ALU.subtract).then_inc(ring_read, 1)
                    dve.wait_ge(ring_read, before + r + 1 + START)
                    nc.vector.tensor_copy(v_next[:, t, :, 1 + C:1 + 2 * C], v_rest[:, k, :, :, :]).then_inc(v2_ready, 1)
                elif item[0] == "chunk":
                    _, n, t, c = item
                    nc.vector.reduce_max(row_max[:, n % 2, t, c:c + 1], bank[:, 0:chunk_width(n, t, c)],
                                         AX.X).then_inc(ring_read, 1)
                    if t == TPB - 1 and c == block_of(n)[1]:
                        dve.wait_ge(ring_read, before + r + 1 + START)
                        nc.vector.tensor_reduce(neg_max[:, n % 2, :], row_max[:, n % 2, :, 0:c + 1], axis=AX.X,
                                                op=ALU.max, negate=True).then_inc(neg_ready, 1)
                else:
                    h, q = block_of(n)
                    r0 = C if h == 0 else 0
                    nc.vector.scalar_tensor_tensor(
                        out=qb[r0:r0 + TPB, h, QB * q:QB * q + QB].rearrange("r (t c) -> r t c", t=TPB),
                        in0=bank[0:TPB, 0:P].unsqueeze(1).to_broadcast([TPB, TPB, P]), scalar=SHIFT,
                        in1=row_sel[:, :, :], op0=ALU.add, op1=ALU.mult).then_inc(ring_read, 1)

            def outputs(it, n):
                dve.wait_ge(slot_used, it * NSLOT + SLOTN[n] + 1 + START)
                h, q = block_of(n)
                dve.wait_ge(z_done, it * NBLK + n + START)
                for k in range(2):
                    z = psum[:, Z + k, 0:2 * VW].rearrange("p (t w) -> p t w", t=2)
                    nc.vector.reciprocal(z_rcp[:, 2 * k:2 * k + 2].unsqueeze(2), z[:, :, 0:1])
                    nc.vector.tensor_reduce(z_sum[:, 2 * k:2 * k + 2, :], z[:, :, 1:VW].rearrange("p t (a c) -> p t c a", a=3),
                                            axis=AX.X, op=ALU.add).then_inc(z_read, 1)
                dve.wait_ge(z_read, (it * NBLK + n) * 2 + 2 + START)
                dve.wait_ge(turned, it * NQ + START)
                nc.vector.tensor_tensor(z_pair[:, TPB * q:TPB * q + TPB, h, :], z_sum[:, :, :],
                                        z_rcp[:, :].unsqueeze(2).to_broadcast([P, TPB, C]), ALU.mult).then_inc(z_done, 1)

            for h, r in ((0, C), (1, 0)):
                nc.vector.memset(qb[r:r + C, h, :].bitcast(F32), 0.0).then_inc(shift_rows, 1)
                nc.vector.memset(kb[r:r + C, h, :].bitcast(F32), 0.0).then_inc(shift_rows, 1)
            dve.wait_ge(shift_rows, 4)
            for h, r in ((0, C), (1, 0)):
                nc.vector.memset(kb[r:r + TPB, h, :].bitcast(F32), 1.0).then_inc(shift_rows, 1)
            dve.wait_ge(consts, CONSTS)

            def split_x(m, u):
                dve.wait_ge(x_hi_done, m * NQ + u + 1)
                dve.wait_ge(proj_ready, m * GROUPS + START)
                nc.vector.tensor_tensor(x_lo[:, :, QB * u:QB * u + QB], x_raw[:, u % 2, :, :],
                                        x_hi[:, :, QB * u:QB * u + QB].bitcast(F32), ALU.subtract).then_inc(x_split, 1)

            def split_w(m):
                dve.wait_ge(w_loaded, m * 16 + 16)
                dve.wait_ge(proj_ready, m * GROUPS + START)
                nc.vector.tensor_copy(w_hi[:, :, :], w_raw[:, :, 0:2 * P]).then_inc(w_hi_done, 1)
                dve.wait_ge(w_hi_done, m + 1)
                nc.vector.tensor_tensor(w_lo[:, :, :], w_raw[:, :, 0:2 * P], w_hi[:, :, :].bitcast(F32),
                                        ALU.subtract).then_inc(w_split, 1)

            def group(m, g):
                kind, u = GROUP_LIST[g]
                bank = psum[:, g % 4, :]
                dve.wait_ge(hi_ready, m * GROUPS + g + 1)
                for h in range(2):
                    src, other = slice(C * h, C * h + C), slice(C - C * h, 2 * C - C * h)
                    cols = slice(QB * u, QB * u + QB)
                    dst = qa[other, h, cols] if kind == "q" else kb[src, h, cols]
                    hi = (qa if kind == "q" else ka)[src, h, cols]
                    last = nc.vector.tensor_tensor(dst, bank[src, :], hi.bitcast(F32), ALU.subtract)
                last.then_inc(proj_read, 1)

            def copy_values(m):
                for u in range(NQ):
                    t = slice(TPB * u, TPB * u + TPB)
                    dve.wait_ge(v_ready, m * NQ + u + 1 + START)
                    nc.vector.tensor_copy(v3[:, t, :, :].rearrange("p t h w -> p (t h w)"),
                                          v_next[:, t, :, :].rearrange("p t h w -> p (t h w)")).then_inc(v_copied, 1)

            def between(it, m):
                for what, *x in BETWEEN:
                    if what == "group" and m is not None:
                        group(m, *x)
                    if what == "ring" and m is not None:
                        ring(RING_0 + m * RING_N, None, *x)
                    if what == "outputs" and it is not None:
                        outputs(it, *x)
                    if what == "values" and m is not None:
                        copy_values(m)

            def pair(it, more):
                for i in range(NSLOT):
                    if more and i - 2 in X_STEPS:
                        split_x(it + 1, X_STEPS.index(i - 2))
                    for what, *x in step_work(i, more):
                        if what == "ring":
                            ring(RING_0 + it * RING_N, it + 1, *x)
                        if what == "outputs":
                            outputs(it, *x)
                    if more and i == W_STEP:
                        split_w(it + 1)
                between(it, it + 1 if more else None)

            for u in range(NQ):
                split_x(0, u)
                ring(0, 0, u, ("values", u))
            split_w(0)
            between(None, 0)
            over_pairs(dve, pair)

        @block.tensor
        def _(pe):
            for started in (turned, proj_ready, slot_used):
                pe.sem_inc(started, START)
            def group(m, g, first=False):
                if g < 4:
                    pe.wait_ge(probs_ready, (m * NSLOT - (1 if g < 2 else 0) if not first else 0) + START)
                else:
                    pe.wait_ge(proj_read, m * GROUPS + g - 3 + START)
                kind, u = GROUP_LIST[g]
                cols, w = slice(QB * u, QB * u + QB), slice(P * "qk".index(kind), P * "qk".index(kind) + P)
                terms = [(a[:, d, w], c[:, d, cols]) for d in range(DT) for a, c in ((w_hi, x_hi), (w_hi, x_lo), (w_lo, x_hi))]
                for k, (lhsT, rhs) in enumerate(terms):
                    last = nc.tensor.matmul(psum[:, g % 4, :], lhsT, rhs, start=(k == 0), stop=(k == len(terms) - 1))
                last.then_inc(proj_ready, 1)

            def ring(before, m, r, item):
                pe.wait_ge(ring_read, before + max(0, r - 1) + START)
                bank = psum[:, RING + r % 2, :]
                if item[0] == "values":
                    u = item[1]
                    pe.wait_ge(w_loaded, m * 16 + 16)
                    pe.wait_ge(x_loaded[u % 2], m * 32 + 16 * (u // 2) + 16)
                    for t in range(TPB):
                        for d in range(DT):
                            last = nc.tensor.matmul(bank[:, P * t:P * t + P], x_raw[:, u % 2, d, P * t:P * t + P],
                                                    w_raw[:, d, 2 * P:3 * P], start=(d == 0), stop=(d == DT - 1))
                elif item[0] == "chunk":
                    _, n, t, c = item
                    h, q = block_of(n)
                    w = chunk_width(n, t, c)
                    tile = TPB * q + t
                    diagonal = c == q
                    last = nc.tensor.matmul(bank[:, 0:w], qa[:, h, P * tile:P * tile + P], ka[:, h, QB * c:QB * c + w],
                                            start=True, stop=not diagonal)
                    if diagonal:
                        last = nc.tensor.matmul(bank[:, w - P:w], ident_b[:, :], mask_q[:, :], start=False, stop=True)
                else:
                    n = item[1]
                    pe.wait_ge(neg_ready, m * NBLK + n + 1)
                    last = nc.tensor.transpose(bank[0:TPB, 0:P], neg_max[:, n % 2, :], ident[:, :])
                last.then_inc(ring_ready, 1)

            def scores(it, i, u, more):
                n, s = SLOTS[i]
                h, q = block_of(n)
                if u == 0:
                    pe.wait_ge(probs_ready, it * NSLOT + max(0, i - 1) + START)
                _, k, f = slot_tiles(n, s)[u]
                cols = slice(QB * q + P * f, QB * q + QB)
                bank = psum[:, 2 * (i % 2) + u, :]
                nc.tensor.matmul(bank[:, P * f:QB], ka[:, h, P * k:P * k + P], qa[:, h, cols], start=True, stop=False)
                if s == 0 and u == 0:
                    pe.wait_ge(ring_read, RING_0 + it * RING_N + TURN_AT[more][n] + 1 + START)
                last = nc.tensor.matmul(bank[:, P * f:QB], kb[:, h, P * k:P * k + P], qb[:, h, cols],
                                        start=False, stop=k < TPB * q)
                if k >= TPB * q:
                    last = nc.tensor.matmul(bank[:, P * f:P * f + P], ident_b[:, :], mask_k[:, :], start=False, stop=True)
                if u == 1:
                    last.then_inc(scores_ready, 1)

            def products(it, i, u):
                n, s = SLOTS[i]
                h, q = block_of(n)
                if u == 0:
                    pe.wait_ge(probs_split, it * NSLOT + i + 1 + START)
                _, k, f = slot_tiles(n, s)[u]
                for t in range(f, TPB):
                    if k == 0 and t % 2 == 0:
                        pe.wait_ge(z_read, (it * NBLK + n) * 2 - (1 - t // 2 if n else 0) + START)
                    z = psum[:, Z + t // 2, VW * (t % 2):VW * (t % 2) + VW]
                    cols = slice(P * t, P * t + P)
                    nc.tensor.matmul(z, p_hi[:, i % NP, u, cols], v3[:, k, h, 0:VW], start=(k == 0 and t % 2 == 0),
                                     stop=False, skip_group_check=True)
                    last = nc.tensor.matmul(z[:, 0:VW - C], p_lo[:, i % NP, u, cols], v3[:, k, h, 0:VW - C],
                                            start=False, stop=(k == TPB * q + t), skip_group_check=True)
                if u == 1:
                    last.then_inc(slot_used, 1)

            def turn_outputs(it, q):
                if q == 0:
                    pe.wait_ge(z_done, it * NBLK + NBLK + START)
                for u in range(TPB):
                    last = nc.tensor.transpose(psum[:, q, P * u:P * u + P],
                                               z_pair[:, TPB * q + u, :, :].rearrange("p h c -> p (h c)"), ident[:, :])
                last.then_inc(turned, 1)

            def between(it, m):
                if m is not None:
                    pe.wait_ge(x_split, m * NQ + NQ + START)
                    pe.wait_ge(w_split, m + 1 + START)
                for what, *x in BETWEEN:
                    if what == "group" and m is not None:
                        group(m, *x, first=it is None)
                    if what == "products" and it is not None:
                        for u in range(2):
                            products(it, *x, u)
                    if what == "ring" and m is not None:
                        if x[0] == 0:
                            pe.wait_ge(proj_read, m * GROUPS + FIRST_GROUPS + START)
                            pe.wait_ge(copies_ready, m * GROUPS * 2 + FIRST_GROUPS * 2 + START)
                        ring(RING_0 + m * RING_N, m, *x)
                    if what == "turned" and it is not None:
                        if m is not None:
                            pe.wait_ge(proj_read, m * GROUPS + GROUPS - NQ + 1 + x[0] + START)
                        else:
                            pe.wait_ge(probs_ready, it * NSLOT + NSLOT + START)
                        turn_outputs(it, *x)

            def pair(it, more):
                pe.wait_ge(proj_read, it * GROUPS + GROUPS + START)
                pe.wait_ge(copies_ready, (it + 1) * GROUPS * 2 + START)
                pe.wait_ge(turned_read, it * NQ + START)
                for i in range(NSLOT):
                    if i == LAG:
                        pe.wait_ge(v_copied, it * NQ + NQ + START)
                    for what, *x in step_work(i, more):
                        if what == "scores":
                            scores(it, *x, more)
                        if what == "products":
                            products(it, *x)
                        if what == "ring":
                            ring(RING_0 + it * RING_N, it + 1 if x[1][0] == "values" else it, *x)
                between(it, it + 1 if more else None)

            for u in range(NQ):
                ring(0, 0, u, ("values", u))
            between(None, 0)
            over_pairs(pe, pair)


def feed_forward(nc, x, zT_dram, wout, b_out, gamma, beta, q1, s1, b1, q2, s2, b2, out):
    with ExitStack() as ctx:
        def sb(name, shape, dt=F32):
            return ctx.enter_context(nc.sbuf_tensor(name, shape, dt))

        def sem(name):
            return ctx.enter_context(nc.semaphore(name))

        identF = sb("identF", [P, P])
        wo = sb("wo", [P, PAIRS, D])
        w1 = sb("w1", [P, DT, F])
        w2 = sb("w2", [P, FT, D])
        q1s, q2s = sb("q1s", [P, DT, F], I32), sb("q2s", [P, FT, D], I32)
        s1s, s2s = sb("s1s", [P, DT, F]), sb("s2s", [P, FT, D])
        bo_s, b2_s, hb2 = sb("bo_s", [P, D]), sb("b2_s", [P, D]), sb("hb2", [P, D])
        gam, bet, b1_s = sb("gam", [P, DT]), sb("bet", [P, DT]), sb("b1_s", [P, FT])
        zT = sb("zT", [P, 2, PAIRS, QB])
        xs = sb("xs", [P, 2, TPB, D])
        y = sb("y", [P, TPB, D])
        ya = sb("ya", [P, TPB, D])
        x1 = sb("x1", [P, TPB, D])
        xn = sb("xn", [P, TPB, D])
        base = sb("base", [P, 2, TPB, D])
        hT = sb("hT", [P, DT, QB])
        aT = sb("aT", [P, FT, QB])
        o = sb("o", [P, TPB, D])
        res = sb("res", [P, 2, TPB, D])
        stats, mv, var_e, std, rstd = (sb(n, s) for n, s in (("stats", [P, TPB, 6]), ("mv", [P, TPB, 2]),
                                                             ("var_e", [P, TPB]), ("std", [P, TPB]), ("rstd", [P, TPB])))
        psum = ctx.enter_context(nc.psum_tensor("psum2", [P, 8, QB], F32))
        WO, HT, FC, ZO = 0, 2, 4, 6

        passed = sem("passed")
        w_in, idF = sem("w_in"), sem("idF")
        zx_in = [sem("zx_in0"), sem("zx_in1")]
        wo_ready, wo_read = sem("wo_ready"), sem("wo_read")
        first_norms, last_norm = sem("first_norms"), sem("last_norm")
        weights = sem("weights")
        norm_ready, hT_ps, hT_ready = sem("norm_ready"), sem("hT_ps"), sem("hT_ready")
        var_ready, std_ready = sem("var_ready"), sem("std_ready")
        fc1_ready, act_ready = sem("fc1_ready"), sem("act_ready")
        fc2_ready, fc2_read = sem("fc2_ready"), sem("fc2_read")
        res_ready = sem("res_ready")
        stored = [sem("stored0"), sem("stored1")]
        block = ctx.enter_context(nc.Block())

        x_blk = x.rearrange("b (q t p) d -> (b q) p t d", t=TPB, p=P)
        out_blk = out.rearrange("b (q t p) d -> (b q) p t d", t=TPB, p=P)

        @block.sync
        def _(sp):
            for started in (stored[0], stored[1]):
                sp.sem_inc(started, START)
            def load(i, k):
                sp.dma_start(zT[:, k, :, :], zT_dram[bass.ds(i, 1), :, :, :].rearrange("i p g t -> (i p) g t")).then_inc(zx_in[k], 16)
                sp.dma_start(xs[:, k, :, :], x_blk[bass.ds(i, 1), :, :, :].rearrange("i p t d -> (i p) t d")).then_inc(zx_in[k], 16)
            load(0, 0)
            sp.dma_start(wo[:, :, :], wout).then_inc(w_in, 16)
            load(1, 1)
            sp.dma_start(q1s[:, :, :], q1.rearrange("(k p) f -> p k f", p=P)).then_inc(w_in, 16)
            sp.dma_start(q2s[:, :, :], q2.rearrange("(k p) f -> p k f", p=P)).then_inc(w_in, 16)
            for k in range(DT):
                sp.dma_start(s1s[:, k, :], s1[k:k + 1, :].to_broadcast([P, F])).then_inc(w_in, 16)
            for k in range(FT):
                sp.dma_start(s2s[:, k, :], s2[k:k + 1, :].to_broadcast([P, D])).then_inc(w_in, 16)
            sp.dma_start(bo_s[:, :], b_out.unsqueeze(0).to_broadcast([P, D])).then_inc(w_in, 16)
            sp.dma_start(b2_s[:, :], b2.unsqueeze(0).to_broadcast([P, D])).then_inc(w_in, 16)
            sp.dma_start(gam[:, :], gamma).then_inc(w_in, 16)
            sp.dma_start(bet[:, :], beta).then_inc(w_in, 16)
            sp.dma_start(b1_s[:, :], b1).then_inc(w_in, 16)
            def store(i, k):
                sp.wait_ge(res_ready, i + 1)
                sp.dma_start(out_blk[bass.ds(i, 1), :, :, :].rearrange("i p t d -> (i p) t d"),
                             res[:, k, :, :]).then_inc(stored[k], 16)
            with sp.Fori(0, TOKB // 2 - 1) as j:
                for k in range(2):
                    store(2 * j + k, k)
                    load(2 * j + k + 2, k)
            for k in range(2):
                store(TOKB - 2 + k, k)
            for k in range(2):
                sp.wait_ge(stored[k], 16 * (TOKB // 2) + START)
        W_IN = 16 * (3 + DT + FT + 5)

        @block.gpsimd
        def _(pool):
            nc.gpsimd.memset(identF[:, :], 0.0).then_inc(idF, 1)
            pool.wait_ge(idF, 1)
            nc.gpsimd.affine_select(out=identF[:, :], in_=identF[:, :], compare_op=ALU.not_equal, fill=1.0, base=0,
                                    pattern=[[-1, P]], channel_multiplier=1).then_inc(idF, 1)

        def over_blocks(eng, step):
            with eng.Fori(0, TOKB // 2 - 1) as j:
                for k in range(2):
                    step(2 * j + k, k, True)
            step(TOKB - 2, 0, True)
            step(TOKB - 1, 1, False)

        @block.tensor
        def _(pe):
            for started in (hT_ps, fc1_ready, fc2_ready):
                pe.sem_inc(started, START)
            def out_projection(i, k):
                pe.wait_ge(zx_in[k], 32 * ((i - k) // 2 + 1) if isinstance(i, int) else (i - k) * 16 + 32)
                pe.wait_ge(wo_read, i + START)
                for t in range(TPB):
                    for g in range(PAIRS):
                        last = nc.tensor.matmul(psum[:, WO + t // 2, D * (t % 2):D * (t % 2) + D],
                                                zT[:, k, g, P * t:P * t + P], wo[:, g, :], start=(g == 0), stop=(g == PAIRS - 1))
                last.then_inc(wo_ready, 1)

            def step(i, k, more):
                pe.wait_ge(norm_ready, i + 1)
                pe.wait_ge(hT_ready, i + START)
                for d in range(DT):
                    for t in range(TPB):
                        last = nc.tensor.transpose(psum[:, HT + d, P * t:P * t + P], xn[:, t, P * d:P * d + P], identF[:, :])
                last.then_inc(hT_ps, 1)
                pe.wait_ge(hT_ready, i + 1 + START)
                for f in range(FT):
                    pe.wait_ge(act_ready, i * FT + max(0, f - 1) + START)
                    for d in range(DT):
                        last = nc.tensor.matmul(psum[:, FC + f % 2, :], w1[:, d, P * f:P * f + P], hT[:, d, :],
                                                start=(d == 0), stop=(d == DT - 1))
                    last.then_inc(fc1_ready, 1)
                if more:
                    out_projection(i + 1, 1 - k)
                pe.wait_ge(act_ready, i * FT + FT + START)
                pe.wait_ge(fc2_read, i + START)
                for t in range(TPB):
                    for f in range(FT):
                        last = nc.tensor.matmul(psum[:, ZO + t // 2, D * (t % 2):D * (t % 2) + D],
                                                aT[:, f, P * t:P * t + P], w2[:, f, :], start=(f == 0), stop=(f == FT - 1))
                last.then_inc(fc2_ready, 1)

            pe.wait_ge(w_in, W_IN)
            pe.wait_ge(idF, 2)
            out_projection(0, 0)
            pe.wait_ge(weights, 2)
            over_blocks(pe, step)

        @block.scalar
        def _(act):
            for started in (act_ready,):
                act.sem_inc(started, START)
            def root(n):
                act.wait_ge(var_ready, n + 1)
                nc.scalar.activation(std[:, :], var_e[:, :], ACT.Sqrt).then_inc(std_ready, 1)

            def step(i, k, more):
                for f in range(FT):
                    act.wait_ge(fc1_ready, i * FT + f + 1 + START)
                    act.wait_ge(fc2_ready, i + START)
                    nc.scalar.activation(aT[:, f, :], psum[:, FC + f % 2, :], ACT.Silu, bias=b1_s[:, f:f + 1]).then_inc(act_ready, 1)
                if more:
                    root(3 * i + 2)
                    root(3 * i + 3)
                    root(3 * i + 4)
                else:
                    root(3 * i + 2)

            act.wait_ge(w_in, W_IN)
            root(0)
            root(1)
            over_blocks(act, step)

        @block.vector
        def _(dve):
            for started in (wo_read, fc2_read, hT_ready):
                dve.sem_inc(started, START)
            class Chain:
                def __init__(self, sem, at):
                    self.sem, self.at = sem, at

                def done(self, instruction):
                    self.at = self.at + 1
                    instruction.then_inc(self.sem, 1)
                    dve.wait_ge(self.sem, self.at)

            def normalise(chain, src, dst, n):
                for t in range(TPB):
                    last = nc.vector.bn_stats(stats[:, t, :], src[:, t, :])
                chain.done(last)
                dve.sem_inc(passed, 1)
                for t in range(TPB):
                    last = nc.vector.bn_aggr(mv[:, t, :], stats[:, t, :])
                chain.done(last)
                nc.vector.tensor_scalar(var_e[:, :], mv[:, :, 1], EPS, None, ALU.add).then_inc(var_ready, 1)
                dve.wait_ge(std_ready, n + 1)
                chain.done(nc.vector.reciprocal(rstd[:, :], std[:, :]))
                for t in range(TPB):
                    last = nc.vector.tensor_scalar(dst[:, t, :], src[:, t, :], mv[:, t, 0:1], rstd[:, t:t + 1],
                                                   ALU.subtract, ALU.mult)
                return last

            NORMS, LAST = 9, 3

            def to_norms(i, k, n):
                chain = Chain(first_norms, i * NORMS)
                dve.wait_ge(wo_ready, i + 1)
                sums = psum[:, WO:WO + 2, :].rearrange("p k (t d) -> p (k t) d", t=2)
                nc.vector.tensor_tensor(y[:, :, :], sums, xs[:, k, :, :], ALU.add).then_inc(wo_read, 1)
                dve.wait_ge(wo_read, i + 1 + START)
                chain.done(nc.vector.tensor_tensor(ya[:, :, :], y[:, :, :], bo_s[:, :].unsqueeze(1).to_broadcast([P, TPB, D]), ALU.add))
                chain.done(normalise(chain, ya, x1, n))
                dve.wait_ge(hT_ps, i + START)
                last = normalise(chain, x1, xn, n + 1)
                last.then_inc(norm_ready, 1)
                nc.vector.scalar_tensor_tensor(out=base[:, k, :, :], in0=x1[:, :, :], scalar=2.0,
                                               in1=hb2[:, :].unsqueeze(1).to_broadcast([P, TPB, D]),
                                               op0=ALU.mult, op1=ALU.add).then_inc(first_norms, 1)
                assert isinstance(i, int) is False or chain.at + 1 == i * NORMS + NORMS, chain.at

            def step(i, k, more):
                dve.wait_ge(hT_ps, i + 1 + START)
                dve.wait_ge(fc1_ready, i * FT + START)
                for d in range(DT):
                    last = nc.vector.tensor_scalar(hT[:, d, :], psum[:, HT + d, :], gam[:, d:d + 1], bet[:, d:d + 1],
                                                   ALU.mult, ALU.add)
                last.then_inc(hT_ready, 1)
                if more:
                    to_norms(i + 1, 1 - k, 3 * i + 2)
                chain = Chain(last_norm, i * LAST)
                dve.wait_ge(fc2_ready, i + 1 + START)
                dve.wait_ge(first_norms, i * NORMS + NORMS)
                sums = psum[:, ZO:ZO + 2, :].rearrange("p k (t d) -> p (k t) d", t=2)
                nc.vector.scalar_tensor_tensor(out=o[:, :, :], in0=sums, scalar=0.5, in1=base[:, k, :, :],
                                               op0=ALU.mult, op1=ALU.add).then_inc(fc2_read, 1)
                dve.wait_ge(fc2_read, i + 1 + START)
                dve.wait_ge(stored[k], (((i - k) // 2) * 16 if isinstance(i, int) else (i - k) * 8) + START)
                last = normalise(chain, o, res[:, k, :, :], 3 * i + 4 if more else 3 * i + 2)
                last.then_inc(res_ready, 1)

            dve.wait_ge(w_in, W_IN)
            nc.vector.scalar_tensor_tensor(out=w1[:, :, :], in0=q1s[:, :, :], scalar=-128.0, in1=s1s[:, :, :],
                                           op0=ALU.add, op1=ALU.mult).then_inc(weights, 1)
            nc.vector.scalar_tensor_tensor(out=w2[:, :, :], in0=q2s[:, :, :], scalar=-128.0, in1=s2s[:, :, :],
                                           op0=ALU.add, op1=ALU.mult).then_inc(weights, 1)
            nc.vector.tensor_scalar(hb2[:, :], b2_s[:, :], 0.5, None, ALU.mult).then_inc(weights, 1)
            dve.wait_ge(weights, 3)
            to_norms(0, 0, 0)
            over_blocks(dve, step)


def build(nc, x, xT, wqkv, wout, b_out, gamma, beta, q1, s1, b1, q2, s2, b2, out):
    zT_dram = nc.dram_tensor("zT_dram", [TOKB, P, PAIRS, QB], F32, kind="Internal").ap()
    attention(nc, xT, wqkv, zT_dram)
    feed_forward(nc, x, zT_dram, wout, b_out, gamma, beta, q1, s1, b1, q2, s2, b2, out)


def kernel(**inputs):
    import numpy as np
    import concourse.bacc as bacc
    from concourse.bass_utils import run_bass_kernel_spmd as run

    a = {n.removeprefix("L0_"): np.asarray(v) for n, v in inputs.items()}
    x = a["attn_resid"]
    xT = x.reshape(B, S, DT, P).transpose(0, 3, 2, 1)
    w = np.stack([a["attn_W_Q"], a["attn_W_K"], a["attn_W_V"]]).reshape(3, DT, P, PAIRS, 2 * C)
    wqkv = w.transpose(3, 2, 1, 0, 4).reshape(PAIRS, P, DT, 3 * P)
    wout = a["attn_W_out"].reshape(C, PAIRS, 2, D).transpose(2, 0, 1, 3).reshape(P, PAIRS, D)
    arrays = {
        "x": x, "xT": xT, "wqkv": wqkv, "wout": wout, "b_out": a["attn_b_out"],
        "gamma": a["ffn_ln_gamma"].reshape(DT, P).T, "beta": a["ffn_ln_beta"].reshape(DT, P).T,
        "q1": a["ffn_fc1_q"], "s1": a["ffn_fc1_scales"], "b1": a["ffn_fc1_bias"].reshape(FT, P).T,
        "q2": a["ffn_fc2_q"], "s2": a["ffn_fc2_scales"], "b2": a["ffn_fc2_bias"],
    }
    arrays = {f"{n}_dram": np.ascontiguousarray(v) for n, v in arrays.items()}
    nc = bacc.Bacc("TRN2", target_bir_lowering=False, num_devices=1)
    d = {n.removesuffix("_dram"): nc.dram_tensor(n, v.shape, mybir.dt.from_np(v.dtype), kind="ExternalInput").ap()
         for n, v in arrays.items()}
    out = nc.dram_tensor("out_dram", (B, S, D), F32, kind="ExternalOutput").ap()
    build(nc, out=out, **d)
    r = run(nc, [arrays], core_ids=[0])
    return r.results[0]["out_dram"]
```

```python
from contextlib import ExitStack

import concourse.bass as bass
from concourse import mybir

F32 = mybir.dt.float32
F32R = mybir.dt.float32r
BF16 = mybir.dt.bfloat16
F16 = mybir.dt.float16
I32 = mybir.dt.int32
ALU = mybir.AluOpType
ACT = mybir.ActivationFunctionType
AX = mybir.AxisListType

P = 128
B, S, D = 2, 2048, 256
H, C = 16, 64
F, G = 1024, 128
DT = D // P
FT = F // P
PAIRS = H // 2
ST = S // P
QB = 512
NQ = S // QB
NBLK = 2 * NQ
TPB = QB // P
VW = 3 * C + 1
VS = VW + 1
START = 1
LAG = 3
NP = 5
NEG = -1.0e30
EPS = 1e-5
SCALE = C ** -0.5
SHIFT = 5.545177444479562 / SCALE
TOKB = B * NQ


Q_ORDER = [0, 1, 2, 3]


def block_of(n):
    return n % 2, Q_ORDER[n // 2]


SLOTS = [(n, s) for n in range(NBLK) for s in range(2 * (block_of(n)[1] + 1))]
SLOT0 = [min(i for i, (m, _) in enumerate(SLOTS) if m == n) for n in range(NBLK)]
SLOTN = [max(i for i, (m, _) in enumerate(SLOTS) if m == n) for n in range(NBLK)]
NSLOT = len(SLOTS)


def chunks_of(n):
    q = block_of(n)[1]
    return [("chunk", n, t, c) for c in range(q + 1) for t in range(TPB)]


def chunk_width(n, t, c):
    return QB if c < block_of(n)[1] else P * (t + 1)


def slot_tiles(n, s):
    first = TPB * block_of(n)[1]
    keys = (2 * s, 2 * s + 1) if 2 * s < first else (first, first + 3) if 2 * s == first else (first + 1, first + 2)
    return [(i, k, max(0, k - first)) for i, k in enumerate(keys)]


def last_slot_tile(n, t):
    return max((n, s, i) for m, s in SLOTS if m == n for i, _, f in slot_tiles(n, s) if f <= t)


GROUP_LIST = [("q", 0), ("q", 1), ("q", 2), ("k", 0), ("k", 1), ("k", 2), ("q", 3), ("k", 3)]
GROUPS = len(GROUP_LIST)
EARLY, LATE = {27: 0, 29: 1, 31: 2, 34: 3, 36: 4, 38: 5}, {0: 6, 1: 7}
X_STEPS, W_STEP = [7, 11, 15, 19], 23
LOAD_STEPS = [3, 3, X_STEPS[0] + 3, X_STEPS[1] + 3]
FIRST_MAXIMA, TAIL_MAXIMA = {37: 3, 38: 3, 39: 3}, [2, 2, 1]
AHEAD_SLOTS, TAIL_SCORES = 2, [0, 2, 2]
DVE_SHARE = 0.80
AHEAD_BLOCKS = 2
MAXES = 4
BANKS = 3


def step_base(i):
    pe = 0.43 * sum(TPB - f for _, _, f in slot_tiles(*SLOTS[i])) / TPB
    dve = 0.0
    if i >= LAG:
        pe += 0.14 * sum(TPB - f for _, _, f in slot_tiles(*SLOTS[i - LAG]))
        if i - LAG in SLOTN:
            dve += 1.5
    groups = (i in EARLY) + (i in LATE)
    pe, dve = pe + 1.3 * groups, dve + 1.3 * groups
    pe, dve = pe + 0.2 * FIRST_MAXIMA.get(i, 0), dve + 0.6 * FIRST_MAXIMA.get(i, 0)
    if i in X_STEPS:
        pe, dve = pe + 1.8, dve + 1.8
    if i - 2 in X_STEPS:
        dve += 1.2
    if i == W_STEP:
        dve += 1.0
    return pe, dve


def chunk_cost(x):
    return 0.08 + 0.00105 * chunk_width(*x[1:])


def first_maxima():
    chunks, turns = chunks_of(0) + chunks_of(1) + chunks_of(2), []
    order = []
    for x in chunks:
        order.append(x)
        if turns and order[-3] == chunks_of(turns[0])[-1]:
            order.append(("turn", turns.pop(0)))
        if x == chunks_of(x[1])[-1]:
            turns.append(x[1])
    return order[:sum(FIRST_MAXIMA.values()) + sum(TAIL_MAXIMA)]


def spread_chunks():
    steps = [[] for _ in SLOTS]
    waiting = [x for n in range(NBLK) for x in chunks_of(n) if x not in first_maxima()]
    credit = 0.0
    time = [step_base(i)[0] for i in range(NSLOT)]
    for i in range(NSLOT):
        need = max([sum(chunk_cost(x) for x in waiting if x[1] <= n) * time[i] / sum(time[i:SLOT0[n] - 2])
                    for n in range(1, NBLK) if SLOT0[n] - 2 > i] + [0.0])
        credit = min(credit, 0.3) + DVE_SHARE * time[i] - step_base(i)[1]
        done = 0.0
        while waiting and waiting[0][1] <= SLOTS[i][0] + AHEAD_BLOCKS:
            cost = chunk_cost(waiting[0])
            if done + cost / 2 > max(need, credit):
                break
            steps[i].append(waiting.pop(0))
            done += cost
        credit -= done
    for n in range(NBLK):
        if ("turn", n) in first_maxima():
            continue
        last = max([i for i, step in enumerate(steps) if chunks_of(n)[-1] in step] + [-1])
        assert last < SLOT0[n] - 2, (n, last)
        steps[last + 1].append(("turn", n))
    return steps


def pair_order(more):
    def step(work, ring):
        out = []
        for k, x in enumerate(work):
            out += [x] + ring[-(-len(ring) * k // len(work)):-(-len(ring) * (k + 1) // len(work))]
        return out

    first = [(x[0], 1, *x[1:]) for x in first_maxima()] if more else []
    order = []
    spread = spread_chunks()
    for i in range(NSLOT):
        ring = [(x[0], 0, *x[1:]) for kind in ("turn", "chunk") for x in spread[i] if x[0] == kind]
        ring += [("group", 0, LATE[i])] if i in LATE else []
        if more:
            ring += [("group", 1, EARLY[i])] if i in EARLY else []
            k = FIRST_MAXIMA.get(i, 0)
            ring, first = ring + first[:k], first[k:]
            ring += [("values", 1, X_STEPS.index(i))] if i in X_STEPS else []
            order += [("load_x", 1, u) for u, at in enumerate(LOAD_STEPS) if i == at]
            if i == LOAD_STEPS[0]:
                order.append(("load_w", 1))
        work = [("scores", 0, i, 0), ("scores", 0, i, 1)] if i >= AHEAD_SLOTS else []
        work += [("products", 0, i - LAG, 0), ("products", 0, i - LAG, 1)] if i >= LAG else []
        order += step(work, ring) if work else ring
        if i - LAG in SLOTN:
            order.append(("outputs", 0, SLOTN.index(i - LAG)))
        if more:
            order += [("x_hi", 1, u) for u, at in enumerate(X_STEPS) if i == at]
            order += [("x_lo", 1, u) for u, at in enumerate(X_STEPS) if i - 2 == at]
            order += [("w", 1)] if i == W_STEP else []
        order += [("out", 0, block_of(n)[1]) for n in range(1, NBLK, 2) if SLOTN[n] + LAG + 2 == i]
    ahead = [("scores", 1, i, u) for i in range(AHEAD_SLOTS) for u in range(2)] if more else []
    for k, i in enumerate(range(NSLOT - LAG, NSLOT)):
        order += [("products", 0, i, 0), ("products", 0, i, 1)]
        if i in SLOTN:
            order.append(("outputs", 0, SLOTN.index(i)))
        order += first[:TAIL_MAXIMA[k]]
        first = first[TAIL_MAXIMA[k]:]
        order += ahead[:TAIL_SCORES[k]]
        ahead = ahead[TAIL_SCORES[k]:]
    order += first + ahead
    if more:
        order.append(("copy_v", 1))
    order += [("out", 0, block_of(n)[1]) for n in range(1, NBLK, 2) if SLOTN[n] + LAG + 2 >= NSLOT]
    return order + [("store", 0)]


def first_order():
    order = [("load_w", 1)] + [("load_x", 1, 0), ("load_x", 1, 1)]
    for u in range(NQ):
        order += [("x_hi", 1, u), ("x_lo", 1, u), ("values", 1, u)]
        if u + 2 < NQ:
            order.append(("load_x", 1, u + 2))
    order += [("w", 1), ("copy_v", 1)] + [("group", 1, g) for g in EARLY.values()]
    order += [(x[0], 1, *x[1:]) for x in first_maxima()]
    return order + [("scores", 1, i, u) for i in range(AHEAD_SLOTS) for u in range(2)]


def placed(order, r=0, a=0):
    out = []
    for what, ahead, *x in order:
        if what in ("chunk", "turn", "values", "group"):
            out.append((what, ahead, r, x))
            r += 1
        elif what in ("scores", "out"):
            out.append((what, ahead, a, x))
            a += 1
        else:
            out.append((what, ahead, None, x))
    return out, r, a


ORDER = {}
ORDER[True], RING_N, LANE_N = placed(pair_order(True))
ORDER[False], _, LANE_END = placed(pair_order(False))
_, RING_0, LANE_0 = placed(first_order())
FIRST, _, _ = placed(first_order(), RING_N - RING_0, LANE_N - LANE_0)
LATE_AT = max(p for what, ahead, p, _ in ORDER[True] if what == "group" and not ahead)


def place_of(order, what, ahead, *x):
    return max([p + 1 for w, a, p, y in order if (w, a, *y) == (what, ahead, *x)] + [0])


def to_be_read(r, base, n):
    last = base + (r - BANKS if r >= BANKS else max(k for k in range(n) if k % BANKS == r % BANKS) - n)
    return max(0, last + 1) if isinstance(base, int) else last + 1


def attention(nc, shared, early_in, xT, wqkv, zT_dram, wout):
    with ExitStack() as ctx:
        def sb(name, shape, dt=F32):
            return ctx.enter_context(nc.sbuf_tensor(name, shape, dt))

        def sem(name):
            return ctx.enter_context(nc.semaphore(name))

        ident = sb("ident", [P, P])
        ident_b = sb("ident_b", [P, P], BF16)
        mask_q = sb("mask_q", [P, P], BF16)
        mask_k = sb("mask_k", [P, P], BF16)
        row_sel = sb("row_sel", [TPB, TPB, P])
        qa = sb("qa", [P, 2, S], F32R)
        qb = sb("qb", [P, 2, S], F32R)
        ka = sb("ka", [P, 2, S], F32R)
        kb = sb("kb", [P, 2, S], F32R)
        x_raw = shared[1][:, 0:2 * DT * QB].rearrange("p (k d t) -> p k d t", k=2, d=DT)
        x_hi = sb("x_hi", [P, DT, S], F32R)
        x_lo = sb("x_lo", [P, DT, S], F32R)
        w_raw = sb("w_raw", [P, DT, 3 * P])
        w_hi = sb("w_hi", [P, DT, 2 * P], F32R)
        w_lo = sb("w_lo", [P, DT, 2 * P], F32R)
        v3 = sb("v3", [P, ST, 2, VS], BF16)
        v_next = shared[0][:, 0:ST * VS].bitcast(BF16).rearrange("p (t h w) -> p t h w", t=ST, h=2)
        v_rest = sb("v_rest", [P, 2, TPB, 2, C])
        p_full = sb("p_full", [P, NP, 2, QB])
        p_hi = sb("p_hi", [P, NP, 2, QB], F16)
        p_lo = sb("p_lo", [P, NP, 2, QB], F16)
        row_max = sb("row_max", [P, MAXES, TPB, NQ])
        neg_max = sb("neg_max", [P, 2, TPB])
        z_rcp = sb("z_rcp", [P, TPB])
        z_sum = sb("z_sum", [P, TPB, C])
        z_pair = sb("z_pair", [P, ST, 2, C])
        z_T = sb("z_T", [P, NQ, QB])
        psum = ctx.enter_context(nc.psum_tensor("psum", [P, 8, QB], F32))
        LANE, RING, Z = 0, BANKS, 2 * BANKS

        passed = sem("passed")
        consts = sem("consts")
        shift_rows = sem("shift_rows")
        x_loaded, w_loaded = [sem("x_loaded0"), sem("x_loaded1")], sem("w_loaded")
        x_hi_done, x_split = sem("x_hi_done"), sem("x_split")
        w_hi_done, w_split = sem("w_hi_done"), sem("w_split")
        hi_ready = sem("hi_ready")
        copied = [sem("copied0"), sem("copied1")]
        v1_ready, v2_ready, v_ready = sem("v1_ready"), sem("v2_ready"), sem("v_ready")
        v_copied = sem("v_copied")
        lane_ready, lane_read = sem("lane_ready"), sem("lane_read")
        ring_ready, ring_read = sem("ring_ready"), sem("ring_read")
        neg_ready = sem("neg_ready")
        probs_split = sem("probs_split")
        slot_used = sem("slot_used")
        z_read = sem("z_read")
        z_done = sem("z_done")
        z_stored = sem("z_stored")
        block = ctx.enter_context(nc.Block())

        USED = NP + START
        CONSTS, COPIED = 12, 32 * (GROUPS // 2)

        def over_pairs(eng, pair):
            with eng.Fori(0, B * PAIRS - 1) as it:
                pair(it, True)
            pair(B * PAIRS - 1, False)

        def ring_base(it):
            return RING_0 + it * RING_N

        def lane_base(it):
            return LANE_0 + it * LANE_N

        def slot_views(i, u, *tensors):
            tiles = slot_tiles(*SLOTS[i])
            if u is None:
                return [tuple(t[:, i % NP, k, P * f:QB] for t in tensors) for k, _, f in tiles] if tiles[1][2] else \
                       [tuple(t[:, i % NP, :, :] for t in tensors)]
            return tuple(t[:, i % NP, u, P * tiles[u][2]:QB] for t in tensors)

        @block.sync
        def _(sp):
            for started in (z_stored, v_copied):
                sp.sem_inc(started, START)

            def load_w(m):
                sp.wait_ge(w_split, m + START)
                sp.sem_inc(passed, 1)
                sp.wait_ge(v1_ready, m * NQ + START)
                sp.sem_inc(passed, 1)
                sp.dma_start(w_raw[:, :, :], wqkv[bass.ds(m % PAIRS, 1), :, :, :].rearrange("g p d n -> (g p) d n")).then_inc(w_loaded, 16)

            def load_x(m, u):
                sp.wait_ge(x_split, m * NQ + max(0, u - 1) + START)
                sp.wait_ge(v1_ready, m * NQ + max(0, u - 1) + START)
                sp.sem_inc(passed, 1)
                sp.dma_start(x_raw[:, u % 2, :, :],
                             xT[bass.ds(m // PAIRS, 1), :, :, QB * u:QB * u + QB].rearrange("b p d s -> (b p) d s")
                             ).then_inc(x_loaded[u % 2], 16)

            def copy_group(m, g):
                kind, u = GROUP_LIST[g]
                cols = slice(QB * u, QB * u + QB)
                sp.wait_ge(copied[g % 2], m * COPIED + 32 * (g // 2) + START)
                for h in range(2):
                    sp.sem_inc(passed, 1)
                    sp.wait_ge(hi_ready, (m * GROUPS + g) * 2 + h + 1)
                    sp.sem_inc(passed, 1)
                    src, other = slice(C * h, C * h + C), slice(C - C * h, 2 * C - C * h)
                    a = (qa if kind == "q" else ka)[src, h, cols]
                    dst = qb[src, h, cols] if kind == "q" else ka[other, h, cols]
                    sp.dma_start(dst.bitcast(F32), a.bitcast(F32)).then_inc(copied[g % 2], 16)

            def pair(it, more, order):
                for what, ahead, _, x in order:
                    m = it + ahead
                    if what == "load_w":
                        load_w(m)
                    if what == "load_x":
                        load_x(m, *x)
                    if what == "group":
                        copy_group(m, *x)
                    if what == "copy_v":
                        sp.wait_ge(v_ready, m * NQ + NQ + START)
                        sp.sem_inc(passed, 1)
                        sp.wait_ge(slot_used, m * NSLOT + USED)
                        sp.dma_start(v3[:, :, :, :], v_next[:, :, :, :]).then_inc(v_copied, 16)
                    if what == "store" and not more:
                        sp.wait_ge(v_copied, 16 * B * PAIRS + START)
                        sp.wait_ge(x_split, NQ * B * PAIRS + START)
                        sp.dma_start(shared[0][:, :].rearrange("p (g t) -> p g t", g=PAIRS), zT_dram[0]).then_inc(early_in, 16)
                        sp.dma_start(shared[1][:, :].rearrange("p (g d) -> p g d", g=PAIRS), wout).then_inc(early_in, 16)
                    if what == "store":
                        sp.wait_ge(lane_read, lane_base(it) + (LANE_N if more else LANE_END) + START)
                        sp.sem_inc(passed, 1)
                        sp.dma_start(zT_dram[bass.ds((m // PAIRS) * NQ, NQ), :, bass.ds(m % PAIRS, 1), :].rearrange("q p g t -> p q (g t)"),
                                     z_T[:, :, :]).then_inc(z_stored, 16)

            sp.sem_inc(copied[0], START)
            sp.sem_inc(copied[1], START)
            sp.wait_ge(consts, CONSTS)
            pair(-1, True, FIRST)
            over_pairs(sp, lambda it, more: pair(it, more, ORDER[more]))
            sp.wait_ge(z_stored, 16 * B * PAIRS + START)

        @block.gpsimd
        def _(pool):
            for started in (probs_split, v_ready):
                pool.sem_inc(started, START)
            nc.gpsimd.memset(ident[:, :], 0.0).then_inc(consts, 1)
            nc.gpsimd.memset(ident_b[:, :], 0.0).then_inc(consts, 1)
            nc.gpsimd.memset(mask_q[:, :], 0.0).then_inc(consts, 1)
            nc.gpsimd.memset(mask_k[:, :], 0.0).then_inc(consts, 1)
            nc.gpsimd.memset(row_sel[:, :, :], 0.0).then_inc(consts, 1)
            nc.gpsimd.memset(v_next[:, :, :, 0:1], 1.0).then_inc(consts, 1)
            nc.gpsimd.memset(v_next[:, :, :, VW:VS], 0.0).then_inc(consts, 1)
            pool.wait_ge(consts, 7)
            for m in (ident, ident_b):
                nc.gpsimd.affine_select(out=m[:, :], in_=m[:, :], compare_op=ALU.not_equal, fill=1.0, base=0,
                                        pattern=[[-1, P]], channel_multiplier=1).then_inc(consts, 1)
            nc.gpsimd.affine_select(out=mask_q[:, :], in_=mask_q[:, :], compare_op=ALU.is_ge, fill=NEG, base=0,
                                    pattern=[[-1, P]], channel_multiplier=1).then_inc(consts, 1)
            nc.gpsimd.affine_select(out=mask_k[:, :], in_=mask_k[:, :], compare_op=ALU.is_ge, fill=NEG, base=0,
                                    pattern=[[1, P]], channel_multiplier=-1).then_inc(consts, 1)
            nc.gpsimd.affine_select(out=row_sel[:, :, :], in_=row_sel[:, :, :], compare_op=ALU.not_equal, fill=1.0,
                                    base=0, pattern=[[-1, TPB], [0, P]], channel_multiplier=1).then_inc(consts, 1)

            def values(m, u):
                t = slice(TPB * u, TPB * u + TPB)
                pool.wait_ge(v2_ready, m * NQ + u + 1)
                for h in range(2):
                    last = nc.gpsimd.tensor_tensor(v_next[:, t, h, 1 + 2 * C:1 + 3 * C], v_rest[:, u % 2, :, h, :],
                                                   v_next[:, t, h, 1 + C:1 + 2 * C], ALU.subtract)
                last.then_inc(v_ready, 1)

            def pair(it, more, order, base):
                for what, ahead, a, x in order:
                    if what == "scores" and x[1] == 1:
                        i = x[0]
                        pool.wait_ge(lane_read, base + a + 1 + START)
                        for dst, full, hi in slot_views(i, None, p_lo, p_full, p_hi):
                            last = nc.gpsimd.tensor_tensor(dst, full, hi, ALU.subtract)
                        last.then_inc(probs_split, 1)
                    if what == "values":
                        values(it + ahead, *x)

            pair(-1, True, FIRST, lane_base(-1))
            over_pairs(pool, lambda it, more: pair(it, more, ORDER[more], lane_base(it)))

        @block.scalar
        def _(act):
            act.sem_inc(lane_read, START)

            def x_high(m, u):
                act.wait_ge(x_loaded[u % 2], m * 32 + 16 * (u // 2) + 16)
                nc.scalar.activation(x_hi[:, :, QB * u:QB * u + QB], x_raw[:, u % 2, :, :], ACT.Copy).then_inc(x_hi_done, 1)

            def group(base, r, m, g):
                kind, u = GROUP_LIST[g]
                act.wait_ge(ring_ready, base + r + 1)
                bank = psum[:, RING + r % BANKS, :]
                for h in range(2):
                    rows = slice(C * h, C * h + C)
                    last = nc.scalar.activation((qa if kind == "q" else ka)[rows, h, QB * u:QB * u + QB], bank[rows, :], ACT.Copy)
                    last.then_inc(hi_ready, 1)

            def pair(it, more, order, base, lane):
                for what, ahead, place, x in order:
                    if what == "scores":
                        i, u = x
                        if u == 0 and order is not FIRST:
                            act.wait_ge(slot_used, (it + ahead) * NSLOT + i - NP + 1 + USED)
                        act.wait_ge(lane_ready, lane + place + 1 + START)
                        hi, full = slot_views(i, u, p_hi, p_full)
                        scores = psum[:, LANE + place % BANKS, P * slot_tiles(*SLOTS[i])[u][2]:QB]
                        nc.scalar.activation(hi, scores, ACT.Exp, scale=SCALE)
                        nc.scalar.activation(full, scores, ACT.Exp, scale=SCALE).then_inc(lane_read, 1)
                    if what == "out":
                        act.wait_ge(z_stored, it * 16 + START)
                        act.wait_ge(lane_ready, lane + place + 1 + START)
                        nc.scalar.activation(z_T[:, x[0], :], psum[:, LANE + place % BANKS, :], ACT.Copy).then_inc(lane_read, 1)
                    if what == "x_hi":
                        if x[0] == 0 and ahead and order is not FIRST:
                            act.wait_ge(ring_ready, base + LATE_AT + 1)
                        x_high(it + ahead, *x)
                    if what == "group":
                        group(base, place, it + ahead, *x)

            pair(-1, True, FIRST, ring_base(-1), lane_base(-1))
            over_pairs(act, lambda it, more: pair(it, more, ORDER[more], ring_base(it), lane_base(it)))

        @block.vector
        def _(dve):
            for started in (x_split, w_split, ring_read, z_done, z_read, v1_ready):
                dve.sem_inc(started, START)
            def ring(base, r, m, what, *x):
                dve.wait_ge(ring_ready, base + r + 1)
                bank = psum[:, RING + r % BANKS, :]
                if what == "values":
                    u, k = x[0], x[0] % 2
                    t = slice(TPB * u, TPB * u + TPB)
                    v = bank.rearrange("p (t h c) -> p t h c", t=TPB, h=2)
                    dve.wait_ge(v_copied, m * 16 + START)
                    nc.vector.tensor_copy(v_next[:, t, :, 1:1 + C], v).then_inc(v1_ready, 1)
                    dve.wait_ge(v_ready, m * NQ + max(0, u - 1) + START)
                    dve.wait_ge(v1_ready, m * NQ + u + 1 + START)
                    nc.vector.tensor_tensor(v_rest[:, k, :, :, :], v,
                                            v_next[:, t, :, 1:1 + C], ALU.subtract).then_inc(ring_read, 1)
                    dve.wait_ge(ring_read, base + r + 1 + START)
                    nc.vector.tensor_copy(v_next[:, t, :, 1 + C:1 + 2 * C], v_rest[:, k, :, :, :]).then_inc(v2_ready, 1)
                if what == "chunk":
                    n, t, c = x
                    nc.vector.reduce_max(row_max[:, n % MAXES, t, c:c + 1], bank[:, 0:chunk_width(n, t, c)],
                                         AX.X).then_inc(ring_read, 1)
                    if ("chunk", *x) == chunks_of(n)[-1]:
                        dve.wait_ge(ring_read, base + r + 1 + START)
                        nc.vector.tensor_reduce(neg_max[:, n % 2, :], row_max[:, n % MAXES, :, 0:block_of(n)[1] + 1],
                                                axis=AX.X, op=ALU.max, negate=True).then_inc(neg_ready, 1)
                if what == "turn":
                    h, q = block_of(x[0])
                    r0 = C if h == 0 else 0
                    nc.vector.scalar_tensor_tensor(
                        out=qb[r0:r0 + TPB, h, QB * q:QB * q + QB].rearrange("r (t c) -> r t c", t=TPB),
                        in0=bank[0:TPB, 0:P].unsqueeze(1).to_broadcast([TPB, TPB, P]), scalar=SHIFT,
                        in1=row_sel[:, :, :], op0=ALU.add, op1=ALU.mult).then_inc(ring_read, 1)
                if what == "group":
                    kind, u = GROUP_LIST[x[0]]
                    for h in range(2):
                        dve.wait_ge(hi_ready, (m * GROUPS + x[0]) * 2 + h + 1)
                        src, other = slice(C * h, C * h + C), slice(C - C * h, 2 * C - C * h)
                        cols = slice(QB * u, QB * u + QB)
                        dst = qa[other, h, cols] if kind == "q" else kb[src, h, cols]
                        hi = (qa if kind == "q" else ka)[src, h, cols]
                        last = nc.vector.tensor_tensor(dst, bank[src, :], hi.bitcast(F32), ALU.subtract)
                    last.then_inc(ring_read, 1)

            def outputs(it, n):
                dve.wait_ge(slot_used, it * NSLOT + SLOTN[n] + 1 + USED)
                h, q = block_of(n)
                dve.wait_ge(z_done, it * NBLK + n + START)
                for k in range(2):
                    z = psum[:, Z + k, 0:2 * VW].rearrange("p (t w) -> p t w", t=2)
                    nc.vector.reciprocal(z_rcp[:, 2 * k:2 * k + 2].unsqueeze(2), z[:, :, 0:1])
                    nc.vector.tensor_reduce(z_sum[:, 2 * k:2 * k + 2, :], z[:, :, 1:VW].rearrange("p t (a c) -> p t c a", a=3),
                                            axis=AX.X, op=ALU.add).then_inc(z_read, 1)
                dve.wait_ge(z_read, (it * NBLK + n) * 2 + 2 + START)
                dve.wait_ge(lane_ready, lane_base(it) + START)
                nc.vector.tensor_tensor(z_pair[:, TPB * q:TPB * q + TPB, h, :], z_sum[:, :, :],
                                        z_rcp[:, :].unsqueeze(2).to_broadcast([P, TPB, C]), ALU.mult).then_inc(z_done, 1)

            for h, r in ((0, C), (1, 0)):
                nc.vector.memset(qb[r:r + C, h, :].bitcast(F32), 0.0).then_inc(shift_rows, 1)
                nc.vector.memset(kb[r:r + C, h, :].bitcast(F32), 0.0).then_inc(shift_rows, 1)
            dve.wait_ge(shift_rows, 4)
            for h, r in ((0, C), (1, 0)):
                nc.vector.memset(kb[r:r + TPB, h, :].bitcast(F32), 1.0).then_inc(shift_rows, 1)
            dve.wait_ge(consts, CONSTS)

            def x_low(m, u):
                dve.wait_ge(x_hi_done, m * NQ + u + 1)
                nc.vector.tensor_tensor(x_lo[:, :, QB * u:QB * u + QB], x_raw[:, u % 2, :, :],
                                        x_hi[:, :, QB * u:QB * u + QB].bitcast(F32), ALU.subtract).then_inc(x_split, 1)

            def split_w(m):
                dve.wait_ge(w_loaded, m * 16 + 16)
                nc.vector.tensor_copy(w_hi[:, :, :], w_raw[:, :, 0:2 * P]).then_inc(w_hi_done, 1)
                dve.wait_ge(w_hi_done, m + 1)
                nc.vector.tensor_tensor(w_lo[:, :, :], w_raw[:, :, 0:2 * P], w_hi[:, :, :].bitcast(F32),
                                        ALU.subtract).then_inc(w_split, 1)

            def pair(it, more, order, base):
                for what, ahead, place, x in order:
                    if what in ("values", "chunk", "turn", "group"):
                        ring(base, place, it + ahead, what, *x)
                    if what == "outputs":
                        outputs(it, *x)
                    if what == "x_lo":
                        x_low(it + ahead, *x)
                    if what == "w":
                        split_w(it + ahead)

            pair(-1, True, FIRST, ring_base(-1))
            over_pairs(dve, lambda it, more: pair(it, more, ORDER[more], ring_base(it)))

        @block.tensor
        def _(pe):
            pe.sem_inc(lane_ready, START)
            pe.sem_inc(slot_used, USED)

            def ring(order, base, r, m, what, ahead, *x):
                pe.wait_ge(ring_read, to_be_read(r, base, RING_N) + START)
                bank = psum[:, RING + r % BANKS, :]
                if what == "group":
                    g = x[0]
                    if g == 0:
                        pe.wait_ge(x_split, m * NQ + NQ + START)
                        pe.wait_ge(w_split, m + 1 + START)
                    kind, u = GROUP_LIST[g]
                    cols, w = slice(QB * u, QB * u + QB), slice(P * "qk".index(kind), P * "qk".index(kind) + P)
                    terms = [(a[:, d, w], c[:, d, cols]) for d in range(DT) for a, c in ((w_hi, x_hi), (w_hi, x_lo), (w_lo, x_hi))]
                    for k, (lhsT, rhs) in enumerate(terms):
                        last = nc.tensor.matmul(bank, lhsT, rhs, start=(k == 0), stop=(k == len(terms) - 1))
                if what == "values":
                    u = x[0]
                    pe.wait_ge(w_loaded, m * 16 + 16)
                    pe.wait_ge(x_loaded[u % 2], m * 32 + 16 * (u // 2) + 16)
                    for t in range(TPB):
                        for d in range(DT):
                            last = nc.tensor.matmul(bank[:, P * t:P * t + P], x_raw[:, u % 2, d, P * t:P * t + P],
                                                    w_raw[:, d, 2 * P:3 * P], start=(d == 0), stop=(d == DT - 1))
                if what == "chunk":
                    n, t, c = x
                    h, q = block_of(n)
                    w = chunk_width(n, t, c)
                    tile = TPB * q + t
                    diagonal = c == q
                    if t == 0 and h == 0:
                        g = max(GROUP_LIST.index(("q", q)), GROUP_LIST.index(("k", c)))
                        pe.wait_ge(ring_read, base + place_of(order, "group", ahead, g) + START)
                        for k in (g - 1, g):
                            pe.wait_ge(copied[k % 2], m * COPIED + 32 * (k // 2 + 1) + START)
                    last = nc.tensor.matmul(bank[:, 0:w], qa[:, h, P * tile:P * tile + P], ka[:, h, QB * c:QB * c + w],
                                            start=True, stop=not diagonal)
                    if diagonal:
                        last = nc.tensor.matmul(bank[:, w - P:w], ident_b[:, :], mask_q[:, :], start=False, stop=True)
                if what == "turn":
                    n = x[0]
                    pe.wait_ge(neg_ready, m * NBLK + n + 1)
                    last = nc.tensor.transpose(bank[0:TPB, 0:P], neg_max[:, n % 2, :], ident[:, :])
                last.then_inc(ring_ready, 1)

            def scores(order, base, m, lane, a, ahead, i, u):
                n, s = SLOTS[i]
                h, q = block_of(n)
                pe.wait_ge(lane_read, to_be_read(a, lane, LANE_N) + START)
                _, k, f = slot_tiles(n, s)[u]
                cols = slice(QB * q + P * f, QB * q + QB)
                bank = psum[:, LANE + a % BANKS, :]
                nc.tensor.matmul(bank[:, P * f:QB], ka[:, h, P * k:P * k + P], qa[:, h, cols], start=True, stop=False)
                if s == 0 and u == 0:
                    pe.wait_ge(ring_read, base + place_of(order, "turn", ahead, n) + START)
                last = nc.tensor.matmul(bank[:, P * f:QB], kb[:, h, P * k:P * k + P], qb[:, h, cols],
                                        start=False, stop=k < TPB * q)
                if k >= TPB * q:
                    last = nc.tensor.matmul(bank[:, P * f:P * f + P], ident_b[:, :], mask_k[:, :], start=False, stop=True)
                last.then_inc(lane_ready, 1)

            def products(it, i, u):
                n, s = SLOTS[i]
                h, q = block_of(n)
                if u == 0:
                    pe.wait_ge(probs_split, it * NSLOT + i + 1 + START)
                    if i == 0:
                        pe.wait_ge(v_copied, it * 16 + 16 + START)
                _, k, f = slot_tiles(n, s)[u]
                for t in range(f, TPB):
                    if k == 0 and t % 2 == 0:
                        pe.wait_ge(z_read, (it * NBLK + n) * 2 - (1 - t // 2 if n else 0) + START)
                    z = psum[:, Z + t // 2, VW * (t % 2):VW * (t % 2) + VW]
                    cols = slice(P * t, P * t + P)
                    nc.tensor.matmul(z, p_hi[:, i % NP, u, cols], v3[:, k, h, 0:VW], start=(k == 0 and t % 2 == 0),
                                     stop=False, skip_group_check=True)
                    last = nc.tensor.matmul(z[:, 0:VW - C], p_lo[:, i % NP, u, cols], v3[:, k, h, 0:VW - C],
                                            start=False, stop=(n, s, u) == last_slot_tile(n, t), skip_group_check=True)
                if u == 1:
                    last.then_inc(slot_used, 1)

            def turn_outputs(it, lane, a, q):
                pe.wait_ge(z_done, it * NBLK + 2 * Q_ORDER.index(q) + 2 + START)
                pe.wait_ge(lane_read, to_be_read(a, lane, LANE_N) + START)
                for u in range(TPB):
                    last = nc.tensor.transpose(psum[:, LANE + a % BANKS, P * u:P * u + P],
                                               z_pair[:, TPB * q + u, :, :].rearrange("p h c -> p (h c)"), ident[:, :])
                last.then_inc(lane_ready, 1)

            def pair(it, more, order, base, lane):
                for what, ahead, place, x in order:
                    if what in ("values", "chunk", "turn", "group"):
                        ring(order, base, place, it + ahead, what, ahead, *x)
                    if what == "scores":
                        scores(order, base, it + ahead, lane, place, ahead, *x)
                    if what == "products":
                        products(it, *x)
                    if what == "out":
                        turn_outputs(it, lane, place, *x)

            pair(-1, True, FIRST, ring_base(-1), lane_base(-1))
            over_pairs(pe, lambda it, more: pair(it, more, ORDER[more], ring_base(it), lane_base(it)))


def feed_forward(nc, shared, early_in, x, zT_dram, b_out, gamma, beta, q1, s1, b1, q2, s2, b2, out):
    with ExitStack() as ctx:
        def sb(name, shape, dt=F32):
            return ctx.enter_context(nc.sbuf_tensor(name, shape, dt))

        def sem(name):
            return ctx.enter_context(nc.semaphore(name))

        z_raw = shared[0][:, :].rearrange("p (g t) -> p g t", g=PAIRS)
        wo_raw = shared[1][:, :].rearrange("p (g d) -> p g d", g=PAIRS)
        res = shared[1][:, :].rearrange("p (k t d) -> p k t d", k=2, t=TPB)
        z_hi, z_lo = sb("z_hi", [P, PAIRS, QB], F32R), sb("z_lo", [P, PAIRS, QB], F32R)
        identF = sb("identF", [P, P])
        wo_hi, wo_lo = sb("wo_hi", [P, PAIRS, D], F32R), sb("wo_lo", [P, PAIRS, D], F32R)
        w1_hi, w1_lo = sb("w1_hi", [P, DT, F], F32R), sb("w1_lo", [P, DT, F], F32R)
        w2_hi, w2_lo = sb("w2_hi", [P, FT, D], F32R), sb("w2_lo", [P, FT, D], F32R)
        w_full = sb("w_full", [P, DT * F])
        w2_full = w_full[:, :].rearrange("p (k d) -> p k d", k=FT)
        a_hi, a_lo = sb("a_hi", [P, FT, QB], F32R), sb("a_lo", [P, FT, QB], F32R)
        fulls = sb("fulls", [P, DT + 2, QB])
        hT, a_full = fulls[:, 0:DT, :], fulls[:, DT:DT + 2, :]
        sums_y, sums_x = sb("sums_y", [P, 2, TPB, D]), sb("sums_x", [P, 2, TPB, D])
        y, ya, x1, xn = sums_y[:, 0], sums_y[:, 1], sums_x[:, 0], sums_x[:, 1]
        base = sb("base", [P, 2, TPB, D])
        q1s = base[:, :, :, :].rearrange("p k t d -> p (k t d)").bitcast(I32).rearrange("p (k f) -> p k f", k=DT)
        s1s = sums_y[:, :, :, :].rearrange("p a t d -> p (a t d)").rearrange("p (k f) -> p k f", k=DT)
        q2s = shared[1][:, :].bitcast(I32).rearrange("p (k d) -> p k d", k=FT)
        s2s = fulls[:, :, :].rearrange("p a t -> p (a t)").rearrange("p (k d) -> p k d", k=FT)
        bo_s, b2_s, hb2 = sb("bo_s", [P, D]), sb("b2_s", [P, D]), sb("hb2", [P, D])
        gam, bet, b1_s = sb("gam", [P, DT]), sb("bet", [P, DT]), sb("b1_s", [P, FT])
        xs = sb("xs", [P, 2, TPB, D])
        hT_hi, hT_lo = sb("hT_hi", [P, DT, QB], F32R), sb("hT_lo", [P, DT, QB], F32R)
        o = sb("o", [P, TPB, D])
        stats, mv, var_e, std, rstd = (sb(n, s) for n, s in (("stats", [P, TPB, 6]), ("mv", [P, TPB, 2]),
                                                             ("var_e", [P, TPB]), ("std", [P, TPB]), ("rstd", [P, TPB])))
        psum = ctx.enter_context(nc.psum_tensor("psum2", [P, 8, QB], F32))
        WO, HT, FC, ZO = 0, 2, 4, 6

        passed = sem("passed")
        q1_in, q2_in, biases_in, idF = sem("q1_in"), sem("q2_in"), sem("biases_in"), sem("idF")
        z_in, x_in = sem("z_in"), [sem("x_in0"), sem("x_in1")]
        z_hi_done, z_split = sem("z_hi_done"), sem("z_split")
        wo_split, w1_split, w2_split = sem("wo_split"), sem("w1_split"), sem("w2_split")
        w2_high, w2_low = sem("w2_high"), sem("w2_low")
        wo_ready, wo_read = sem("wo_ready"), sem("wo_read")
        first_norms, last_norm = sem("first_norms"), sem("last_norm")
        norm_ready, hT_ps, hT_parts, hT_ready = sem("norm_ready"), sem("hT_ps"), sem("hT_parts"), sem("hT_ready")
        var_ready, std_ready = sem("var_ready"), sem("std_ready")
        fc1_ready, act_ready, a_split = sem("fc1_ready"), sem("act_ready"), sem("a_split")
        fc2_used = sem("fc2_used")
        fc2_read = sem("fc2_read")
        res_ready = sem("res_ready")
        stored = [sem("stored0"), sem("stored1")]
        block = ctx.enter_context(nc.Block())

        x_blk = x.rearrange("b (q t p) d -> (b q) p t d", t=TPB, p=P)
        out_blk = out.rearrange("b (q t p) d -> (b q) p t d", t=TPB, p=P)
        ZQ = 4
        GQ = PAIRS // ZQ
        W_STEPS = 3
        MLAG = 3

        def quarter(t, u):
            return t[:, GQ * u:GQ * u + GQ, :]

        @block.sync
        def _(sp):
            for started in (stored[0], stored[1]):
                sp.sem_inc(started, START)
            def load_z(i):
                sp.wait_ge(z_split, i * ZQ)
                sp.dma_start(z_raw, zT_dram[bass.ds(i, 1), :, :, :].rearrange("i p g t -> (i p) g t")).then_inc(z_in, 16)

            def load_x(i, k):
                sp.dma_start(xs[:, k, :, :], x_blk[bass.ds(i, 1), :, :, :].rearrange("i p t d -> (i p) t d")).then_inc(x_in[k], 16)

            sp.dma_start(q1s, q1.rearrange("(k p) f -> p k f", p=P)).then_inc(q1_in, 16)
            for k in range(DT):
                sp.dma_start(s1s[:, k, :], s1[k:k + 1, :].to_broadcast([P, F])).then_inc(q1_in, 16)
            sp.dma_start(bo_s[:, :], b_out.unsqueeze(0).to_broadcast([P, D])).then_inc(biases_in, 16)
            sp.dma_start(b2_s[:, :], b2.unsqueeze(0).to_broadcast([P, D])).then_inc(biases_in, 16)
            sp.dma_start(gam[:, :], gamma).then_inc(biases_in, 16)
            sp.dma_start(bet[:, :], beta).then_inc(biases_in, 16)
            sp.dma_start(b1_s[:, :], b1).then_inc(biases_in, 16)
            load_x(0, 0)
            load_z(1)
            sp.wait_ge(wo_split, 2)
            sp.dma_start(q2s, q2.rearrange("(k p) f -> p k f", p=P)).then_inc(q2_in, 16)
            for k in range(FT):
                sp.dma_start(s2s[:, k, :], s2[k:k + 1, :].to_broadcast([P, D])).then_inc(q2_in, 16)
            load_x(1, 1)

            def store(i, k):
                sp.wait_ge(res_ready, i + 1 + START)
                sp.dma_start(out_blk[bass.ds(i, 1), :, :, :].rearrange("i p t d -> (i p) t d"),
                             res[:, k, :, :]).then_inc(stored[k], 16)
            with sp.Fori(0, TOKB // 2 - 1) as j:
                for k in range(2):
                    load_z(2 * j + k + 2)
                    store(2 * j + k, k)
                    load_x(2 * j + k + 2, k)
            for k in range(2):
                store(TOKB - 2 + k, k)
            for k in range(2):
                sp.wait_ge(stored[k], 16 * (TOKB // 2) + START)

        def over_blocks(eng, step):
            with eng.Fori(0, TOKB // 2 - 1) as j:
                for k in range(2):
                    step(2 * j + k, k, 2)
            step(TOKB - 2, 0, 1)
            step(TOKB - 1, 1, 0)

        Z_AT = {4: 0, 5: 1, 6: 2, 7: 3}

        @block.gpsimd
        def _(pool):
            pool.sem_inc(a_split, START)
            nc.gpsimd.memset(identF[:, :], 0.0).then_inc(idF, 1)
            pool.wait_ge(idF, 1)
            nc.gpsimd.affine_select(out=identF[:, :], in_=identF[:, :], compare_op=ALU.not_equal, fill=1.0, base=0,
                                    pattern=[[-1, P]], channel_multiplier=1).then_inc(idF, 1)

            def step(i, k, more):
                for f in range(FT):
                    pool.wait_ge(act_ready, i * FT + f + 1 + START)
                    nc.gpsimd.tensor_tensor(a_lo[:, f, :], a_full[:, f % 2, :], a_hi[:, f, :].bitcast(F32),
                                            ALU.subtract).then_inc(a_split, 1)
            for i in range(2):
                for u in range(ZQ):
                    pool.wait_ge(z_hi_done, i * ZQ + u + 1)
                    nc.gpsimd.tensor_tensor(quarter(z_lo, u), quarter(z_raw, u), quarter(z_hi, u).bitcast(F32),
                                            ALU.subtract).then_inc(z_split, 1)
            pool.wait_ge(w2_high, 1)
            nc.gpsimd.tensor_tensor(w2_lo[:, :, :], w2_full, w2_hi[:, :, :].bitcast(F32), ALU.subtract).then_inc(w2_low, 1)
            over_blocks(pool, step)

        @block.tensor
        def _(pe):
            for started in (fc1_ready, fc2_used):
                pe.sem_inc(started, START)
            def passes(psum_out, stationary, moving, first, last):
                for n, (a, b) in enumerate(((0, 0), (0, 1), (1, 0))):
                    mm = nc.tensor.matmul(psum_out, stationary[a], moving[b], start=first and n == 0, stop=last and n == 2,
                                          skip_group_check=True)
                return mm

            def out_projection(i):
                pe.wait_ge(wo_read, i + START)
                for g in range(PAIRS):
                    if g % GQ == 0:
                        pe.wait_ge(z_split, i * ZQ + g // GQ + 1)
                    for t in range(TPB):
                        cols = slice(P * t, P * t + P)
                        last = passes(psum[:, WO + t // 2, D * (t % 2):D * (t % 2) + D], (z_hi[:, g, cols], z_lo[:, g, cols]),
                                      (wo_hi[:, g, :], wo_lo[:, g, :]), g == 0 and t % 2 == 0, g == PAIRS - 1)
                last.then_inc(wo_ready, 1)

            def turn(i):
                pe.wait_ge(norm_ready, i + 1)
                for d in range(DT):
                    for t in range(TPB):
                        last = nc.tensor.transpose(psum[:, HT + d, P * t:P * t + P], xn[:, t, P * d:P * d + P], identF[:, :])
                last.then_inc(hT_ps, 1)

            def fc1(i, f):
                pe.wait_ge(act_ready, i * FT + max(0, f - 1) + START)
                cols = slice(P * f, P * f + P)
                for d in range(DT):
                    last = passes(psum[:, FC + f % 2, :], (w1_hi[:, d, cols], w1_lo[:, d, cols]), (hT_hi[:, d, :], hT_lo[:, d, :]),
                                  d == 0, d == DT - 1)
                last.then_inc(fc1_ready, 1)

            def fc2(i, f):
                pe.wait_ge(a_split, i * FT + f + 1 + START)
                if f == 0:
                    pe.wait_ge(fc2_read, i + START)
                for t in range(TPB):
                    cols = slice(P * t, P * t + P)
                    last = passes(psum[:, ZO + t // 2, D * (t % 2):D * (t % 2) + D], (a_hi[:, f, cols], a_lo[:, f, cols]),
                                  (w2_hi[:, f, :], w2_lo[:, f, :]), f == 0 and t % 2 == 0, f == FT - 1)
                last.then_inc(fc2_used, 1)

            def step(i, k, more):
                pe.wait_ge(hT_ready, i + 1)
                for f in range(FT + MLAG):
                    if f < FT:
                        fc1(i, f)
                    if f >= MLAG:
                        fc2(i, f - MLAG)
                if more:
                    turn(i + 1)
                if more == 2:
                    out_projection(i + 2)

            pe.wait_ge(idF, 2)
            pe.wait_ge(wo_split, 2)
            out_projection(0)
            out_projection(1)
            turn(0)
            pe.wait_ge(w1_split, W_STEPS)
            pe.wait_ge(w2_low, 1)
            over_blocks(pe, step)

        @block.scalar
        def _(act):
            act.sem_inc(act_ready, START)

            def root(n):
                act.wait_ge(var_ready, n + 1)
                nc.scalar.activation(std[:, :], var_e[:, :], ACT.Sqrt).then_inc(std_ready, 1)

            def split_z(i, u):
                act.wait_ge(z_in, i * 16)
                act.wait_ge(wo_ready, i)
                nc.scalar.activation(quarter(z_hi, u), quarter(z_raw, u), ACT.Copy).then_inc(z_hi_done, 1)

            def step(i, k, more):
                for f in range(FT):
                    act.wait_ge(fc1_ready, i * FT + f + 1 + START)
                    act.wait_ge(fc2_used, i * FT + START)
                    act.wait_ge(a_split, i * FT + max(0, f - 1) + START)
                    for dst in (a_hi[:, f, :], a_full[:, f % 2, :]):
                        last = nc.scalar.activation(dst, psum[:, FC + f % 2, :], ACT.Silu, bias=b1_s[:, f:f + 1])
                    last.then_inc(act_ready, 1)
                    if more == 2 and f in Z_AT:
                        split_z(i + 2, Z_AT[f])
                    if more and f in ROOTS_AT:
                        root(3 * i + 2 + ROOTS_AT.index(f))
                root(3 * i + 4 if more else 3 * i + 2)

            ROOTS_AT = (3, 5)

            act.wait_ge(early_in, 16 * 2)
            for u in range(ZQ):
                nc.scalar.activation(quarter(z_hi, u), quarter(z_raw, u), ACT.Copy).then_inc(z_hi_done, 1)
            for u in range(ZQ):
                split_z(1, u)
            root(0)
            root(1)
            act.wait_ge(w2_split, 2)
            nc.scalar.activation(w2_hi[:, :, :], w2_full, ACT.Copy).then_inc(w2_high, 1)
            act.wait_ge(biases_in, 16 * 5)
            over_blocks(act, step)

        @block.vector
        def _(dve):
            for started in (wo_read, fc2_read, res_ready):
                dve.sem_inc(started, START)
            class Chain:
                def __init__(self, sem, at):
                    self.sem, self.at = sem, at

                def done(self, instruction):
                    self.at = self.at + 1
                    instruction.then_inc(self.sem, 1)
                    dve.wait_ge(self.sem, self.at)

            def split(chain, full, hi, lo):
                chain.done(nc.vector.tensor_copy(hi, full))
                chain.done(nc.vector.tensor_tensor(lo, full, hi.bitcast(F32), ALU.subtract))

            def dequantise(chain, q, scales):
                chain.done(nc.vector.scalar_tensor_tensor(out=w_full[:, :].rearrange("p (k n) -> p k n", k=q.shape[1]), in0=q,
                                                          scalar=-128.0, in1=scales, op0=ALU.add, op1=ALU.mult))

            def normalise(chain, src, dst, n):
                for t in range(TPB):
                    last = nc.vector.bn_stats(stats[:, t, :], src[:, t, :])
                chain.done(last)
                dve.sem_inc(passed, 1)
                for t in range(TPB):
                    last = nc.vector.bn_aggr(mv[:, t, :], stats[:, t, :])
                chain.done(last)
                nc.vector.tensor_scalar(var_e[:, :], mv[:, :, 1], EPS, None, ALU.add).then_inc(var_ready, 1)
                dve.wait_ge(std_ready, n + 1)
                chain.done(nc.vector.reciprocal(rstd[:, :], std[:, :]))
                for t in range(TPB):
                    last = nc.vector.tensor_scalar(dst[:, t, :], src[:, t, :], mv[:, t, 0:1], rstd[:, t:t + 1],
                                                   ALU.subtract, ALU.mult)
                return last

            NORMS, LAST = 9, 3

            def to_norms(i, k, n):
                chain = Chain(first_norms, i * NORMS)
                dve.wait_ge(wo_ready, i + 1)
                dve.wait_ge(x_in[k], 16 * ((i - k) // 2 + 1) if isinstance(i, int) else (i - k) * 8 + 16)
                sums = psum[:, WO:WO + 2, :].rearrange("p k (t d) -> p (k t) d", t=2)
                nc.vector.tensor_tensor(y[:, :, :], sums, xs[:, k, :, :], ALU.add).then_inc(wo_read, 1)
                dve.wait_ge(wo_read, i + 1 + START)
                chain.done(nc.vector.tensor_tensor(ya[:, :, :], y[:, :, :], bo_s[:, :].unsqueeze(1).to_broadcast([P, TPB, D]), ALU.add))
                chain.done(normalise(chain, ya, x1, n))
                last = normalise(chain, x1, xn, n + 1)
                last.then_inc(norm_ready, 1)
                nc.vector.scalar_tensor_tensor(out=base[:, k, :, :], in0=x1[:, :, :], scalar=2.0,
                                               in1=hb2[:, :].unsqueeze(1).to_broadcast([P, TPB, D]),
                                               op0=ALU.mult, op1=ALU.add).then_inc(first_norms, 1)

            def split_z(i):
                for u in range(ZQ):
                    dve.wait_ge(z_hi_done, i * ZQ + u + 1)
                    nc.vector.tensor_tensor(quarter(z_lo, u), quarter(z_raw, u), quarter(z_hi, u).bitcast(F32),
                                            ALU.subtract).then_inc(z_split, 1)

            def to_hT(i):
                dve.wait_ge(hT_ps, i + 1)
                for dst in (hT_hi, hT):
                    for d in range(DT):
                        last = nc.vector.tensor_scalar(dst[:, d, :], psum[:, HT + d, :], gam[:, d:d + 1], bet[:, d:d + 1],
                                                       ALU.mult, ALU.add)
                last.then_inc(hT_parts, 1)
                dve.wait_ge(hT_parts, i + 1)
                nc.vector.tensor_tensor(hT_lo[:, :, :], hT[:, :, :], hT_hi[:, :, :].bitcast(F32), ALU.subtract).then_inc(hT_ready, 1)

            def step(i, k, more):
                if more:
                    to_norms(i + 1, 1 - k, 3 * i + 2)
                    if more == 2:
                        split_z(i + 2)
                    to_hT(i + 1)
                chain = Chain(last_norm, i * LAST)
                dve.wait_ge(fc2_used, i * FT + FT + START)
                dve.wait_ge(first_norms, i * NORMS + NORMS)
                dve.wait_ge(res_ready, i + START)
                sums = psum[:, ZO:ZO + 2, :].rearrange("p k (t d) -> p (k t) d", t=2)
                nc.vector.scalar_tensor_tensor(out=o[:, :, :], in0=sums, scalar=0.5, in1=base[:, k, :, :],
                                               op0=ALU.mult, op1=ALU.add).then_inc(fc2_read, 1)
                dve.wait_ge(fc2_read, i + 1 + START)
                dve.wait_ge(stored[k], (((i - k) // 2) * 16 if isinstance(i, int) else (i - k) * 8) + START)
                last = normalise(chain, o, res[:, k, :, :], 3 * i + 4 if more else 3 * i + 2)
                last.then_inc(res_ready, 1)

            dve.wait_ge(early_in, 16 * 2)
            split(Chain(wo_split, 0), wo_raw, wo_hi[:, :, :], wo_lo[:, :, :])
            dve.wait_ge(q1_in, 16 * (1 + DT))
            chain = Chain(w1_split, 0)
            dequantise(chain, q1s, s1s)
            split(chain, w_full[:, :].rearrange("p (k n) -> p k n", k=DT), w1_hi[:, :, :], w1_lo[:, :, :])
            dve.wait_ge(biases_in, 16 * 5)
            chain = Chain(w2_split, 0)
            chain.done(nc.vector.tensor_scalar(hb2[:, :], b2_s[:, :], 0.5, None, ALU.mult))
            to_norms(0, 0, 0)
            dve.wait_ge(q2_in, 16 * (1 + FT))
            dequantise(Chain(w2_split, 1), q2s, s2s)
            to_hT(0)
            over_blocks(dve, step)


def build(nc, x, xT, wqkv, wout, b_out, gamma, beta, q1, s1, b1, q2, s2, b2, out):
    zT_dram = nc.dram_tensor("zT_dram", [TOKB, P, PAIRS, QB], F32, kind="Internal").ap()
    with ExitStack() as ctx:
        shared = [ctx.enter_context(nc.sbuf_tensor(name, [P, n], F32)) for name, n in (("shared_z", PAIRS * QB), ("shared_w", PAIRS * D))]
        early_in = ctx.enter_context(nc.semaphore("early_in"))
        attention(nc, shared, early_in, xT, wqkv, zT_dram, wout)
        feed_forward(nc, shared, early_in, x, zT_dram, b_out, gamma, beta, q1, s1, b1, q2, s2, b2, out)


def kernel(**inputs):
    import numpy as np
    import concourse.bacc as bacc
    from concourse.bass_utils import run_bass_kernel_spmd as run

    a = {n.removeprefix("L0_"): np.asarray(v) for n, v in inputs.items()}
    x = a["attn_resid"]
    xT = x.reshape(B, S, DT, P).transpose(0, 3, 2, 1)
    w = np.stack([a["attn_W_Q"], a["attn_W_K"], a["attn_W_V"]]).reshape(3, DT, P, PAIRS, 2 * C)
    wqkv = w.transpose(3, 2, 1, 0, 4).reshape(PAIRS, P, DT, 3 * P)
    wout = a["attn_W_out"].reshape(C, PAIRS, 2, D).transpose(2, 0, 1, 3).reshape(P, PAIRS, D)
    arrays = {
        "x": x, "xT": xT, "wqkv": wqkv, "wout": wout, "b_out": a["attn_b_out"],
        "gamma": a["ffn_ln_gamma"].reshape(DT, P).T, "beta": a["ffn_ln_beta"].reshape(DT, P).T,
        "q1": a["ffn_fc1_q"], "s1": a["ffn_fc1_scales"], "b1": a["ffn_fc1_bias"].reshape(FT, P).T,
        "q2": a["ffn_fc2_q"], "s2": a["ffn_fc2_scales"], "b2": a["ffn_fc2_bias"],
    }
    arrays = {f"{n}_dram": np.ascontiguousarray(v) for n, v in arrays.items()}
    nc = bacc.Bacc("TRN2", target_bir_lowering=False, num_devices=1)
    d = {n.removesuffix("_dram"): nc.dram_tensor(n, v.shape, mybir.dt.from_np(v.dtype), kind="ExternalInput").ap()
         for n, v in arrays.items()}
    out = nc.dram_tensor("out_dram", (B, S, D), F32, kind="ExternalOutput").ap()
    build(nc, out=out, **d)
    r = run(nc, [arrays], core_ids=[0])
    return r.results[0]["out_dram"]
```
